# Optimizing a Trainium2 kernel written in Bass

```python
import numpy as np
import jax
import jax.numpy as jnp

def _softmax(x, axis=-1):
    return jax.nn.softmax(x, axis=axis)

def _gelu(x):
    return jax.nn.gelu(x, approximate=True)

def _silu(x):
    return jax.nn.silu(x)

def _sigmoid(x):
    return jax.nn.sigmoid(x)

def _layernorm(x, axis=-1, eps=1e-05):
    m = jnp.mean(x, axis=axis, keepdims=True)
    v = jnp.var(x, axis=axis, keepdims=True)
    return (x - m) / jnp.sqrt(v + eps)

def _scatter_add(tgt, idx, src, axis=0):
    return tgt.at[idx].add(src)

def _segment_sum(src, seg, n):
    return jax.ops.segment_sum(src, seg, n)
kernel_name = 'mk_xattn_ffn_d1_seqx_r8_74f95d'

def setup_inputs(seed: int=0):
    np.random.seed(seed)
    _w = jnp.asarray

    def _rec_inputs():
        import jax
        import jax.numpy as jnp
        _rk = jax.random.key(seed)
        x = -0.000125 + 0.9999 * jax.random.normal(jax.random.fold_in(_rk, 1), (4, 256, 256), jnp.float32)
        _lenS = 256 - jax.random.randint(jax.random.fold_in(_rk, 7), (4,), 0, max(1, 256 // 4) + 1, jnp.int32)
        _lenS2 = 256 - jax.random.randint(jax.random.fold_in(_rk, 8), (4,), 0, max(1, 256 // 4) + 1, jnp.int32)
        itok_BxS_13_99985 = jax.random.randint(jax.random.fold_in(_rk, 11), (4, 256), 13, 99986, jnp.int32)
        _ctx_2048P = jax.random.normal(jax.random.fold_in(_rk, 12), (4, 16, 256), jnp.float32)
        _ctx_2048c = jax.random.dirichlet(jax.random.fold_in(_rk, 512), 0.3 * jnp.ones((16,), jnp.float32), (4, 256))
        _ctx_2048t = jnp.einsum('bsk,bkd->bsd', _ctx_2048c, _ctx_2048P)
        _ctx_2048t = _ctx_2048t * jax.lax.rsqrt(jnp.mean(jnp.square(_ctx_2048t)) + 1e-12) * 0.953939
        ctx_2048 = 6.82029e-06 + 0.0200006 * (_ctx_2048t + 0.3 * jax.random.normal(jax.random.fold_in(_rk, 612), (4, 256, 256), jnp.float32))
        return (x, itok_BxS_13_99985, ctx_2048)
    x, itok_BxS_13_99985, ctx_2048 = _rec_inputs()

    def _L0_xattn_setup():
        import jax, jax.numpy as jnp
        import numpy as np
        B, S, D = (4, 512, 256)
        E = 4
        F = 1024 // E
        VOCAB = 12500
        key = jax.random.key(seed)
        k1, k2, k3, k4, k5 = jax.random.split(key, 5)
        hidden_states = jax.random.normal(k1, (B, S, D), dtype=jnp.float32)
        token_ids = jax.random.randint(k2, (B, S), 0, VOCAB, dtype=jnp.int64)
        Wg = jax.random.normal(k3, (E, F, D), dtype=jnp.float32) * 0.02
        Wu = jax.random.normal(k4, (E, F, D), dtype=jnp.float32) * 0.02
        Wd = jax.random.normal(k5, (E, D, F), dtype=jnp.float32) * 0.02
        return {'hidden_states': hidden_states, 'token_ids': token_ids, 'Wg': Wg, 'Wu': Wu, 'Wd': Wd}
    _L0_xattn_all = _L0_xattn_setup()
    _L0_xattn_in = {k: v for k, v in _L0_xattn_all.items() if k in ()}
    del _L0_xattn_all

    def _L0_ffn_setup():
        import jax, jax.numpy as jnp
        import numpy as np
        TOP_K = 4
        ROUTED_SCALE = 1.0
        NORM_TOPK = True
        B, S, H = (1, 256, 256)
        E, I = (16, 96)
        IS = 96
        key = jax.random.key(seed)
        ks = jax.random.split(key, 8)
        s = 0.02
        return {'hidden_states': jax.random.normal(ks[0], (B, S, H), jnp.float32), 'router_w': jax.random.normal(ks[1], (E, H), jnp.float32) * s, 'e_bias': jax.random.normal(ks[2], (E,), jnp.float32) * s, 'gate_up_proj': jax.random.normal(ks[3], (E, 2 * I, H), jnp.float32) * s, 'down_proj': jax.random.normal(ks[4], (E, H, I), jnp.float32) * s, 'shared_gate_w': jax.random.normal(ks[5], (IS, H), jnp.float32) * s, 'shared_up_w': jax.random.normal(ks[6], (IS, H), jnp.float32) * s, 'shared_down_w': jax.random.normal(ks[7], (H, IS), jnp.float32) * s}
    _L0_ffn_all = _L0_ffn_setup()
    _L0_ffn_in = {k: v for k, v in _L0_ffn_all.items() if k in ('router_w', 'e_bias', 'gate_up_proj', 'down_proj', 'shared_gate_w', 'shared_up_w', 'shared_down_w')}
    del _L0_ffn_all
    return {'x': x, 'itok_BxS_13_99985': itok_BxS_13_99985, 'ctx_2048': ctx_2048, 'L0_ffn_router_w': _L0_ffn_in['router_w'], 'L0_ffn_e_bias': _L0_ffn_in['e_bias'], 'L0_ffn_gate_up_proj': _L0_ffn_in['gate_up_proj'], 'L0_ffn_down_proj': _L0_ffn_in['down_proj'], 'L0_ffn_shared_gate_w': _L0_ffn_in['shared_gate_w'], 'L0_ffn_shared_up_w': _L0_ffn_in['shared_up_w'], 'L0_ffn_shared_down_w': _L0_ffn_in['shared_down_w']}

def reference(x, itok_BxS_13_99985, ctx_2048, L0_ffn_router_w, L0_ffn_e_bias, L0_ffn_gate_up_proj, L0_ffn_down_proj, L0_ffn_shared_gate_w, L0_ffn_shared_up_w, L0_ffn_shared_down_w):
    import jax
    import jax.numpy as jnp

    def _L0_xattn_ref(hidden_states, token_ids, Wg, Wu, Wd):
        import jax, jax.numpy as jnp
        import numpy as np
        B, S, D = (4, 512, 256)
        E = 4
        F = 1024 // E
        VOCAB = 12500
        tokens_per_expert = VOCAB // E
        tid = jnp.clip(token_ids, 0, VOCAB - 1)
        expert_ids = jnp.minimum(tid // tokens_per_expert, E - 1)
        out = jnp.zeros_like(hidden_states)
        for e in range(E):
            g = jax.nn.silu(jnp.einsum('bsd,fd->bsf', hidden_states, Wg[e]))
            u = jnp.einsum('bsd,fd->bsf', hidden_states, Wu[e])
            y = jnp.einsum('bsf,df->bsd', g * u, Wd[e])
            out = jnp.where((expert_ids == e)[..., None], y, out)
        return out

    def _L0_ffn_ref(hidden_states, router_w, e_bias, gate_up_proj, down_proj, shared_gate_w, shared_up_w, shared_down_w):
        import jax, jax.numpy as jnp
        import numpy as np
        TOP_K = 4
        ROUTED_SCALE = 1.0
        NORM_TOPK = True
        B, S, H = (1, 256, 256)
        E, I = (16, 96)
        IS = 96
        orig_shape = hidden_states.shape
        x = hidden_states.reshape(-1, orig_shape[-1])
        T = x.shape[0]
        scores = jax.nn.sigmoid(x @ router_w.T)
        _, topk_idx = jax.lax.top_k(scores + e_bias[None, :], TOP_K)
        topk_w = jnp.take_along_axis(scores, topk_idx, axis=1)
        if NORM_TOPK:
            topk_w = topk_w / (topk_w.sum(axis=-1, keepdims=True) + 1e-20)
        topk_w = topk_w * ROUTED_SCALE
        combine = jnp.zeros((T, E), x.dtype).at[jnp.arange(T)[:, None], topk_idx].add(topk_w)

        def step(acc, xs):
            gu_w, d_w, c = xs
            gu = x @ gu_w.T
            g, u = jnp.split(gu, 2, axis=1)
            y = jax.nn.silu(g) * u @ d_w.T
            return (acc + c[:, None] * y, None)
        routed, _ = jax.lax.scan(step, jnp.zeros_like(x), (gate_up_proj, down_proj, combine.T))
        shared = jax.nn.silu(x @ shared_gate_w.T) * (x @ shared_up_w.T) @ shared_down_w.T
        return (routed + shared).reshape(orig_shape)
    x = x + _L0_xattn_ref(_layernorm(x, axis=-1), itok_BxS_13_99985, ctx_2048, ctx_2048, ctx_2048)
    x = x + _L0_ffn_ref(_layernorm(x, axis=-1), L0_ffn_router_w, L0_ffn_e_bias, L0_ffn_gate_up_proj, L0_ffn_down_proj, L0_ffn_shared_gate_w, L0_ffn_shared_up_w, L0_ffn_shared_down_w)
    return x

_drawn_inputs = setup_inputs


def setup_inputs(seed=0):
    import zlib

    import numpy as np

    out = dict(_drawn_inputs(seed))
    spreads = {}
    factors = {'L0_ffn_router_w': 8.0,
     'L0_ffn_e_bias': 8.0,
     'L0_ffn_gate_up_proj': 8.0,
     'L0_ffn_down_proj': 8.0,
     'L0_ffn_shared_gate_w': 5.543,
     'L0_ffn_shared_up_w': 5.477,
     'L0_ffn_shared_down_w': 5.479}
    for name, (base, spread) in spreads.items():
        noise = np.random.default_rng([zlib.crc32(name.encode()), seed]).standard_normal(out[name].shape)
        drawn = base * np.exp(spread * noise) if base else spread * noise
        out[name] = jnp.asarray(drawn.astype(out[name].dtype))
    for name, factor in factors.items():
        out[name] = (out[name] * factor).astype(out[name].dtype)
    return out
```

```python
from contextlib import ExitStack

import concourse.bass as bass
from concourse import mybir

F32 = mybir.dt.float32
F32R = mybir.dt.float32r
I32 = mybir.dt.int32
U8 = mybir.dt.uint8
ALU = mybir.AluOpType
ACT = mybir.ActivationFunctionType
AX = mybir.AxisListType

P = 128
TOKENS = 1024
D = 256
KC = D // P
HALF = 512
HALVES = TOKENS // HALF
TT = HALF // P
E1 = 4
VOCAB = 12500
PER_EXPERT = VOCAB // E1
EPS = 1e-5

E2 = 16
TOP = 4
I = 96
CH = E2 * I // P
ITEMS = CH + 1
SH = 2 * KC * I
CW = 2 * KC * P
GU = SH + CH * CW
SENTINEL = -3.0e38
MARK = 3.0e38

STAGE = 1024
SLOTS = 3


def weight_pieces():
    pieces = [("ctx", e * KC * D, KC * D) for e in range(E1)]
    pieces += [("gu", 0, SH)] + [("gu", c, STAGE) for c in range(SH, GU, STAGE)]
    pieces += [("sel", c, CH * P // 2) for c in (0, CH * P // 2)]
    pieces += [("wd0", 0, D)] + [("wd", c, STAGE) for c in range(0, CH * D, STAGE)]
    return pieces


def build(nc, x_d, idrow_d, idcol_d, ctx_d, rw_d, bias_d, gu_d, wd0_d, wd_d, sel_d, ident_d, out_d):
    pieces = weight_pieces()
    last_piece = {what: n for n, (what, _, _) in enumerate(pieces)}
    lows = [n for n, (what, _, _) in enumerate(pieces) if what != "sel"]

    with ExitStack() as ctx:
        def sb(name, shape, dt=F32):
            return ctx.enter_context(nc.sbuf_tensor(name, shape, dt))

        def sem(name):
            return ctx.enter_context(nc.semaphore(name))

        x = sb("x", [P, HALVES * TT, D])
        x1t = sb("x1t", [P, KC, TOKENS])
        stage = sb("stage", [P, SLOTS, STAGE])
        ctx_hi = sb("ctx_hi", [P, E1, KC, D], F32R)
        ctx_lo = sb("ctx_lo", [P, E1, KC, D], F32R)
        gu_hi = sb("gu_hi", [P, GU], F32R)
        gu_lo = sb("gu_lo", [P, GU], F32R)
        wd_hi = sb("wd_hi", [P, ITEMS, D], F32R)
        wd_lo = sb("wd_lo", [P, ITEMS, D], F32R)
        sel_r = sb("sel_r", [2 * E2, CH, P], F32R)
        ident = sb("ident", [P, P])
        idrow = sb("idrow", [P, TOKENS], I32)
        idcol = sb("idcol", [P, HALVES * TT], I32)
        gerow = sb("gerow", [P, E1 - 1, TOKENS], U8)
        gecol = sb("gecol", [P, E1 + 1, HALVES * TT])
        pick = sb("pick", [P, E1, HALVES * TT])
        stats = sb("stats", [P, TT, 6])
        meanvar = sb("meanvar", [P, TT, 2])
        vareps = sb("vareps", [P, TT])
        rstd = sb("rstd", [P, TT])
        power = sb("power", [P, TT])
        xn = sb("xn", [P, TT, D])
        xt_hi = sb("xt_hi", [P, HALVES, KC, HALF], F32R)
        xt_lo = sb("xt_lo", [P, HALVES, KC, HALF], F32R)
        act_sb = sb("act_sb", [P, 2, HALF])
        prod = sb("prod", [P, 2, HALF])
        hid = sb("hid", [P, 2, HALF])
        h_hi = sb("h_hi", [P, HALVES, KC, HALF], F32R)
        h_lo = sb("h_lo", [P, HALVES, KC, HALF], F32R)
        rw = sb("rw", [P, KC, E2])
        rw_hi = sb("rw_hi", [P, KC, E2], F32R)
        rw_lo = sb("rw_lo", [P, KC, E2], F32R)
        bias = sb("bias", [P, E2])
        scores = sb("scores", [P, TT, E2])
        biased = sb("biased", [P, TT, E2 + 4])
        best = sb("best", [P, TT, 8])
        marked = sb("marked", [P, TT, E2 + 4])
        chosen = sb("chosen", [P, TT, E2])
        weight = sb("weight", [P, TT, E2])
        wsum = sb("wsum", [P, TT])
        wsume = sb("wsume", [P, TT])
        winv = sb("winv", [P, TT])
        comb = sb("comb", [P, TT, E2])
        comb2 = sb("comb2", [P, TT, 2 * E2])
        combt = sb("combt", [2 * E2, HALVES, HALF], F32R)

        bank = [ctx.enter_context(nc.psum_tensor(f"bank{n}", [P, HALF], F32)) for n in range(8)]
        work = bank[0:4]
        side = bank[4:6]
        acc = bank[6:8]

        x_in = [sem(f"x_in{h}") for h in range(HALVES)]
        slot_in = [sem(f"slot_in{s}") for s in range(SLOTS)]
        idrow_in, idcol_in, small_in, ident_in = sem("idrow_in"), sem("idcol_in"), sem("small_in"), sem("ident_in")
        out_written = sem("out_written")
        w_hi, w_lo = sem("w_hi"), sem("w_lo")
        consts = sem("consts")
        dstep = sem("dstep")
        varied, powered, normed = sem("varied"), sem("powered"), sem("normed")
        side_done = sem("side_done")
        xhi_done, xlo_done = sem("xhi_done"), sem("xlo_done")
        z_done, z_first, z_silu, h1_done = sem("z_done"), sem("z_first"), sem("z_silu"), sem("h1_done")
        z_picked = sem("z_picked")
        y_done, y_added = sem("y_done"), sem("y_added")
        rw_done, scored, combined, combt_done = sem("rw_done"), sem("scored"), sem("combined"), sem("combt_done")
        gate_done, up_done, silu_done, prod_done = sem("gate_done"), sem("up_done"), sem("silu_done"), sem("prod_done")
        c_done, hid_done, hhi_done, hlo_done, down_done = sem("c_done"), sem("hid_done"), sem("hhi_done"), sem("hlo_done"), sem("down_done")
        x1t_done, out_ready = sem("x1t_done"), sem("out_ready")

        side_order = [("n1", 0, 0, 4), ("n1", 0, 1, 5), ("n1", 1, 0, 4), ("n1", 1, 1, 5),
                      ("x1t", 0, 0, 4), ("x1t", 0, 1, 5), ("n2", 0, 0, 4), ("n2", 0, 1, 5),
                      ("router", 0, 0, 5), ("combt", 0, 0, 5),
                      ("n2", 1, 0, 5), ("n2", 1, 1, 5), ("x1t", 1, 0, 5), ("x1t", 1, 1, 5),
                      ("router", 1, 0, 5), ("combt", 1, 0, 5)]
        side_at = {u[:3]: n for n, u in enumerate(side_order)}

        def wait_side_read(eng, b, n):
            before = [u for u in side_order[:n] if u[3] == b]
            if not before:
                return
            what, h, k, _ = before[-1]
            if what in ("n1", "n2"):
                count = (HALVES * KC if what == "n2" else 0) + h * KC + k + 1
                eng.wait_ge(xhi_done, count)
                eng.wait_ge(xlo_done, count)
            elif what == "x1t":
                eng.wait_ge(x1t_done, h * KC + k + 1)
            elif what == "router":
                eng.wait_ge(scored, h + 1)
            else:
                eng.wait_ge(combt_done, h + 1)

        def side_bank(what, h, c):
            return bank[side_order[side_at[what, h, c]][3]]

        def widths(c):
            return I if c == 0 else P

        def gu_cols(c, k, up):
            w = widths(c)
            at = (k * 2 + up) * w + (SH + (c - 1) * CW if c else 0)
            return slice(at, at + w)

        def gu_piece(c):
            return last_piece["ctx"] + 1 + (0 if c == 0 else 1 + (c - 1) * CW // STAGE)

        def wd_piece(c):
            return last_piece["wd0"] + (0 if c == 0 else 1 + (c - 1) * D // STAGE)

        items = [(h, c) for h in range(HALVES) for c in range(ITEMS)]
        N = len(items)

        def hidden_of(g):
            return (prod if items[g][1] == 0 else hid)[0:widths(items[g][1]), g % 2]

        def wait_hidden(eng, g):
            if items[g][1] == 0:
                eng.wait_ge(prod_done, g + 1)
            else:
                eng.wait_ge(hid_done, c_before(g))

        def c_before(g):
            return sum(c > 0 for _, c in items[:g + 1])

        def piece_aps(n):
            what, at, cols = pieces[n]
            st = stage[:, n % SLOTS, 0:cols]
            if what == "ctx":
                e = at // (KC * D)
                st = st.rearrange("p (k f) -> p k f", k=KC)
                return ctx_d[:, e], st, ctx_hi[:, e], ctx_lo[:, e]
            if what == "gu":
                return gu_d[:, at:at + cols], st, gu_hi[:, at:at + cols], gu_lo[:, at:at + cols]
            if what == "sel":
                st = stage[0:2 * E2, n % SLOTS, 0:cols]
                hi = sel_r[:, :, :].rearrange("k c r -> k (c r)")[:, at:at + cols]
                return sel_d[:, at:at + cols], st, hi, None
            if what == "wd0":
                st = stage[0:I, n % SLOTS, 0:cols]
                return wd0_d, st, wd_hi[0:I, 0], wd_lo[0:I, 0]
            hi = wd_hi[:, 1:, :].rearrange("p c d -> p (c d)")[:, at:at + cols]
            lo = wd_lo[:, 1:, :].rearrange("p c d -> p (c d)")[:, at:at + cols]
            return wd_d[:, at:at + cols], st, hi, lo

        block = ctx.enter_context(nc.Block())

        @block.sync
        def _(sp):
            def load_piece(n):
                if n >= SLOTS:
                    sp.wait_ge(w_hi, n - SLOTS + 1)
                    before = sum(m <= n - SLOTS for m in lows)
                    sp.wait_ge(w_lo, before)
                dram, st, _, _ = piece_aps(n)
                sp.dma_start(st, dram).then_inc(slot_in[n % SLOTS], 16)

            sp.dma_start(x[:, 0:TT], x_d[:, 0:TT]).then_inc(x_in[0], 16)
            load_piece(0)
            sp.dma_start(ident[:], ident_d).then_inc(ident_in, 16)
            load_piece(1)
            sp.dma_start(idrow[:], idrow_d.partition_broadcast(P)).then_inc(idrow_in, 16)
            load_piece(2)
            sp.dma_start(x[:, TT:], x_d[:, TT:]).then_inc(x_in[1], 16)
            load_piece(3)
            sp.dma_start(idcol[:], idcol_d).then_inc(idcol_in, 16)
            sp.dma_start(rw[:], rw_d).then_inc(small_in, 16)
            sp.dma_start(bias[:], bias_d.partition_broadcast(P)).then_inc(small_in, 16)
            for n in range(4, len(pieces)):
                load_piece(n)
            for h in range(HALVES):
                for k in range(KC):
                    sp.wait_ge(out_ready, h * KC + k + 1)
                    sp.dma_start(out_d[:, k, h * HALF:(h + 1) * HALF],
                                 x1t[:, k, h * HALF:(h + 1) * HALF]).then_inc(out_written, 16)
            sp.wait_ge(out_written, 16 * HALVES * KC)

        @block.gpsimd
        def _(pool):
            nc.gpsimd.memset(power[:], -0.5).then_inc(consts, 1)
            nc.gpsimd.memset(biased[:, :, E2:], SENTINEL).then_inc(consts, 1)
            pool.wait_ge(consts, 2)

            def low_part(n):
                pool.wait_ge(w_hi, n + 1)
                pool.wait_ge(slot_in[n % SLOTS], 16 * (n // SLOTS + 1))
                _, st, hi, lo = piece_aps(n)
                nc.gpsimd.tensor_tensor(lo, st, hi.bitcast(F32), ALU.subtract).then_inc(w_lo, 1)

            def rstd_of(n):
                pool.wait_ge(varied, n + 1)
                if n > 0:
                    pool.wait_ge(normed, TT * n)
                nc.gpsimd.tensor_tensor(rstd[:], vareps[:], power[:], ALU.pow).then_inc(powered, 1)

            low_part(0)
            rstd_of(0)
            low_part(1)
            low_part(2)
            low_part(3)
            rstd_of(1)
            for n in lows[4:]:
                low_part(n)
            rstd_of(2)
            rstd_of(3)

        @block.scalar
        def _(act):
            def high_part(n):
                act.wait_ge(slot_in[n % SLOTS], 16 * (n // SLOTS + 1))
                _, st, hi, _ = piece_aps(n)
                nc.scalar.activation(hi, st, ACT.Copy).then_inc(w_hi, 1)

            def x_high(what, h, k):
                act.wait_ge(side_done, side_at[what, h, k] + 1)
                if what == "n2":
                    act.wait_ge(z_done, (h + 1) * KC * E1)
                nc.scalar.activation(xt_hi[:, h, k], side_bank(what, h, k)[:], ACT.Copy).then_inc(xhi_done, 1)

            def first_z(h, m):
                n = h * KC + m
                act.wait_ge(z_done, n * E1 + 1)
                if n >= 2:
                    act.wait_ge(h1_done, n - 1)
                nc.scalar.activation(prod[:, n % 2], work[0][:], ACT.Copy).then_inc(z_first, 1)

            def silu_z(h, m):
                n = h * KC + m
                act.wait_ge(z_picked, (n + 1) * (E1 - 1))
                if n >= 2:
                    act.wait_ge(h1_done, n - 1)
                nc.scalar.activation(act_sb[:, n % 2], prod[:, n % 2], ACT.Silu).then_inc(z_silu, 1)

            def residual(h, k):
                u = side_at["x1t", h, k]
                act.wait_ge(side_done, u + 1)
                nc.scalar.activation(x1t[:, k, h * HALF:(h + 1) * HALF], side_bank("x1t", h, k)[:],
                                     ACT.Copy).then_inc(x1t_done, 1)

            def score(h):
                act.wait_ge(side_done, side_at["router", h, 0] + 1)
                if h:
                    act.wait_ge(combined, h)
                nc.scalar.activation(scores[:].rearrange("p t e -> p (t e)"),
                                     side_bank("router", h, 0)[:, 0:TT * E2], ACT.Sigmoid).then_inc(scored, 1)

            def combine_rows(h):
                act.wait_ge(side_done, side_at["combt", h, 0] + 1)
                nc.scalar.activation(combt[:, h], side_bank("combt", h, 0)[0:2 * E2, :], ACT.Copy).then_inc(combt_done, 1)

            def silu_gate(g):
                _, c = items[g]
                w = widths(c)
                act.wait_ge(gate_done, g + 1)
                if g >= 2:
                    act.wait_ge(prod_done, g - 1)
                else:
                    act.wait_ge(h1_done, HALVES * KC)
                nc.scalar.activation(act_sb[0:w, g % 2], work[2 * (g % 2)][0:w, :], ACT.Silu).then_inc(silu_done, 1)

            def hid_high(g):
                _, c = items[g]
                w = widths(c)
                wait_hidden(act, g)
                if g >= 4:
                    act.wait_ge(down_done, g - 3)
                elif g == 0:
                    act.wait_ge(y_done, HALVES * TT)
                nc.scalar.activation(h_hi[0:w, (g // 2) % 2, g % 2], hidden_of(g), ACT.Copy).then_inc(hhi_done, 1)

            nc.scalar.preload_act_table(ACT.Silu)
            high_part(0)
            high_part(1)
            x_high("n1", 0, 0)
            x_high("n1", 0, 1)
            high_part(2)
            high_part(3)
            first_z(0, 0)
            x_high("n1", 1, 0)
            x_high("n1", 1, 1)
            silu_z(0, 0)
            first_z(0, 1)
            high_part(4)
            silu_z(0, 1)
            high_part(5)
            first_z(1, 0)
            high_part(6)
            silu_z(1, 0)
            high_part(7)
            first_z(1, 1)
            high_part(8)
            silu_z(1, 1)
            for n in range(9, 13):
                high_part(n)
            for n in range(13, len(pieces)):
                high_part(n)
            residual(0, 0)
            residual(0, 1)
            x_high("n2", 0, 0)
            x_high("n2", 0, 1)
            score(0)
            for g in range(N + 1):
                if g < N:
                    silu_gate(g)
                if g == 2:
                    combine_rows(0)
                if g == 3:
                    x_high("n2", 1, 0)
                if g == 4:
                    x_high("n2", 1, 1)
                if g == 5:
                    residual(1, 0)
                if g == 6:
                    residual(1, 1)
                if g == 8:
                    score(1)
                if g == 12:
                    combine_rows(1)
                if g >= 1:
                    hid_high(g - 1)

        @block.vector
        def _(dve):
            steps = [0]

            def step(ins):
                steps[0] += 1
                ins.then_inc(dstep, 1)
                return steps[0]

            def layer_norm_stats(n, h):
                if n < HALVES:
                    dve.wait_ge(x_in[h], 16)
                for t in range(TT):
                    last = step(nc.vector.bn_stats(stats[:, t], x[:, h * TT + t]))
                    layer_norm_aggr(t, last)

            def layer_norm_aggr(t, after):
                dve.wait_ge(dstep, after)
                step(nc.vector.bn_aggr(meanvar[:, t], stats[:, t]))

            def layer_norm_eps():
                dve.wait_ge(dstep, steps[0])
                nc.vector.tensor_scalar(vareps[:], meanvar[:, :, 1], EPS, None, ALU.add).then_inc(varied, 1)

            def layer_norm_apply(n, h):
                dve.wait_ge(powered, n + 1)
                if n > 0:
                    what, hh = [("n1", 0), ("n1", 1), ("n2", 0)][n - 1]
                    dve.wait_ge(side_done, side_at[what, hh, 1] + 1)
                for t in range(TT):
                    nc.vector.tensor_scalar(xn[:, t], x[:, h * TT + t], meanvar[:, t, 0:1], rstd[:, t:t + 1],
                                            ALU.subtract, ALU.mult).then_inc(normed, 1)

            def x_low(what, h, k):
                n = (HALVES * KC if what == "n2" else 0) + h * KC + k
                dve.wait_ge(xhi_done, n + 1)
                dve.wait_ge(side_done, side_at[what, h, k] + 1)
                nc.vector.tensor_tensor(xt_lo[:, h, k], side_bank(what, h, k)[:], xt_hi[:, h, k].bitcast(F32),
                                        ALU.subtract).then_inc(xlo_done, 1)

            def masks_row(h):
                if h == 0:
                    dve.wait_ge(idrow_in, 16)
                for e in range(1, E1):
                    last = step(nc.vector.tensor_scalar(gerow[:, e - 1, h * HALF:(h + 1) * HALF],
                                                        idrow[:, h * HALF:(h + 1) * HALF],
                                                        float(e * PER_EXPERT), None, ALU.is_ge))
                return last

            def masks_col():
                dve.wait_ge(idcol_in, 16)
                step(nc.vector.memset(gecol[:, 0], 1.0))
                step(nc.vector.memset(gecol[:, E1], 0.0))
                for e in range(1, E1):
                    step(nc.vector.tensor_scalar(gecol[:, e], idcol[:], float(e * PER_EXPERT), None, ALU.is_ge))
                dve.wait_ge(dstep, steps[0])
                return step(nc.vector.tensor_tensor(pick[:], gecol[:, 0:E1], gecol[:, 1:], ALU.subtract))

            def pick_z(h, m, masked):
                n = h * KC + m
                dve.wait_ge(z_first, n + 1)
                dve.wait_ge(dstep, masked)
                for e in range(1, E1):
                    dve.wait_ge(z_done, n * E1 + e + 1)
                    if e > 1:
                        dve.wait_ge(z_picked, n * (E1 - 1) + e - 1)
                    ins = nc.vector.copy_predicated(prod[:, n % 2], gerow[:, e - 1, h * HALF:(h + 1) * HALF], work[e][:])
                    ins.then_inc(z_picked, 1)

            def hidden_1(h, m):
                n = h * KC + m
                dve.wait_ge(z_silu, n + 1)
                last = step(nc.vector.tensor_tensor(hid[:, n % 2], act_sb[:, n % 2], prod[:, n % 2], ALU.mult))
                dve.wait_ge(dstep, last)
                last = step(nc.vector.tensor_scalar(h_hi[:, h, m], hid[:, n % 2], 1.0, None, ALU.mult))
                dve.wait_ge(dstep, last)
                nc.vector.tensor_tensor(h_lo[:, h, m], hid[:, n % 2], h_hi[:, h, m].bitcast(F32),
                                        ALU.subtract).then_inc(h1_done, 1)

            def add_y(h, t, picked):
                T = h * TT + t
                dve.wait_ge(y_done, T + 1)
                dve.wait_ge(dstep, picked)
                for e in range(E1):
                    y = work[2 * (T % 2) + e // 2][:, (e % 2) * D:(e % 2 + 1) * D]
                    ins = nc.vector.scalar_tensor_tensor(out=x[:, T], in0=y, scalar=pick[:, e, T:T + 1],
                                                         in1=x[:, T], op0=ALU.mult, op1=ALU.add)
                    ins.then_inc(y_added, 1)
                    dve.wait_ge(y_added, T * E1 + e + 1)
                last = step(nc.vector.bn_stats(stats[:, t], x[:, T]))
                layer_norm_aggr(t, last)

            def split_router():
                dve.wait_ge(small_in, 32)
                last = step(nc.vector.tensor_scalar(rw_hi[:], rw[:], 1.0, None, ALU.mult))
                dve.wait_ge(dstep, last)
                nc.vector.tensor_tensor(rw_lo[:], rw[:], rw_hi[:].bitcast(F32), ALU.subtract).then_inc(rw_done, 1)

            def route(h):
                dve.wait_ge(scored, h + 1)
                dve.wait_ge(consts, 2)
                if h:
                    dve.wait_ge(side_done, side_at["combt", h - 1, 0] + 1)
                last = step(nc.vector.tensor_tensor(
                    biased[:, :, 0:E2], scores[:], bias[:].unsqueeze(1).to_broadcast([P, TT, E2]), ALU.add))
                dve.wait_ge(dstep, last)
                for t in range(TT):
                    last = step(nc.vector.max(best[:, t], biased[:, t, 0:E2]))
                dve.wait_ge(dstep, last)
                last = step(nc.vector.memset(best[:, :, TOP:], SENTINEL))
                dve.wait_ge(dstep, last)
                for t in range(TT):
                    last = step(nc.vector.match_replace(marked[:, t], best[:, t], biased[:, t], MARK))
                dve.wait_ge(dstep, last)
                last = step(nc.vector.tensor_tensor(chosen[:], marked[:, :, 0:E2], biased[:, :, 0:E2], ALU.is_gt))
                dve.wait_ge(dstep, last)
                last = step(nc.vector.tensor_tensor(weight[:], chosen[:], scores[:], ALU.mult))
                dve.wait_ge(dstep, last)
                last = step(nc.vector.tensor_reduce(wsum[:], weight[:], AX.X, ALU.add))
                dve.wait_ge(dstep, last)
                last = step(nc.vector.tensor_scalar(wsume[:], wsum[:], 1e-20, None, ALU.add))
                dve.wait_ge(dstep, last)
                last = step(nc.vector.reciprocal(winv[:], wsume[:]))
                dve.wait_ge(dstep, last)
                last = step(nc.vector.tensor_tensor(comb[:], weight[:], winv[:].unsqueeze(2).to_broadcast([P, TT, E2]), ALU.mult))
                dve.wait_ge(dstep, last)
                last = step(nc.vector.tensor_scalar(comb2[:, :, 0:E2].bitcast(F32R), comb[:], 1.0, None, ALU.mult))
                dve.wait_ge(dstep, last)
                nc.vector.tensor_tensor(comb2[:, :, E2:], comb[:], comb2[:, :, 0:E2], ALU.subtract).then_inc(combined, 1)

            def product(g):
                _, c = items[g]
                w = widths(c)
                dve.wait_ge(silu_done, g + 1)
                dve.wait_ge(up_done, g + 1)
                if g >= 2 and items[g - 2][1] == 0:
                    dve.wait_ge(hhi_done, g - 1)
                    dve.wait_ge(hlo_done, g - 1)
                elif g >= 2:
                    dve.wait_ge(hid_done, c_before(g - 2))
                nc.vector.tensor_tensor(prod[0:w, g % 2], act_sb[0:w, g % 2], work[2 * (g % 2) + 1][0:w, :],
                                        ALU.mult).then_inc(prod_done, 1)

            def hidden_2(g):
                _, c = items[g]
                if c == 0:
                    return
                dve.wait_ge(prod_done, g + 1)
                dve.wait_ge(c_done, c_before(g))
                if g >= 2:
                    dve.wait_ge(hhi_done, g - 1)
                    dve.wait_ge(hlo_done, g - 1)
                nc.vector.tensor_tensor(hid[:, g % 2], prod[:, g % 2], bank[4][:], ALU.mult).then_inc(hid_done, 1)

            def hid_low(g):
                _, c = items[g]
                w = widths(c)
                dve.wait_ge(hhi_done, g + 1)
                nc.vector.tensor_tensor(h_lo[0:w, (g // 2) % 2, g % 2], hidden_of(g),
                                        h_hi[0:w, (g // 2) % 2, g % 2].bitcast(F32), ALU.subtract).then_inc(hlo_done, 1)

            def output(h):
                dve.wait_ge(down_done, (h + 1) * ITEMS)
                dve.wait_ge(x1t_done, (h + 1) * KC)
                for k in range(KC):
                    o = x1t[:, k, h * HALF:(h + 1) * HALF]
                    nc.vector.tensor_tensor(o, acc[k][:], o, ALU.add).then_inc(out_ready, 1)

            layer_norm_stats(0, 0)
            layer_norm_eps()
            masked0 = masks_row(0)
            layer_norm_apply(0, 0)
            x_low("n1", 0, 0)
            x_low("n1", 0, 1)
            layer_norm_stats(1, 1)
            layer_norm_eps()
            masked1 = masks_row(1)
            picked = masks_col()
            layer_norm_apply(1, 1)
            split_router()
            pick_z(0, 0, masked0)
            x_low("n1", 1, 0)
            x_low("n1", 1, 1)
            hidden_1(0, 0)
            for h, m in ((0, 1), (1, 0), (1, 1)):
                pick_z(h, m, masked1)
                hidden_1(h, m)
            for t in range(TT):
                add_y(0, t, picked)
            layer_norm_eps()
            layer_norm_apply(2, 0)
            for t in range(TT):
                add_y(1, t, picked)
                if t == 2:
                    x_low("n2", 0, 0)
                    x_low("n2", 0, 1)
            layer_norm_eps()
            layer_norm_apply(3, 1)
            route(0)
            for g in range(N + 1):
                if g == ITEMS + 2:
                    output(0)
                if g < N:
                    product(g)
                if g == 3:
                    x_low("n2", 1, 0)
                if g == 4:
                    x_low("n2", 1, 1)
                if g == 9:
                    route(1)
                if g >= 1:
                    hidden_2(g - 1)
                    hid_low(g - 1)
            output(1)

        @block.tensor
        def _(pe):
            def side_wait(what, h, c):
                u = side_at[what, h, c]
                b = side_order[u][3]
                wait_side_read(pe, b, u)
                return bank[b]

            def split_product(out, lhs, rhs, first, last):
                for n, (a, b) in enumerate(((0, 0), (0, 1), (1, 0))):
                    ins = nc.tensor.matmul(out, lhs[a], rhs[b], start=(first and n == 0), stop=(last and n == 2))
                return ins

            def transposes(what, h, k, src):
                b = side_wait(what, h, k)
                for t in range(TT):
                    ins = nc.tensor.transpose(b[:, t * P:(t + 1) * P], src[:, t, k * P:(k + 1) * P], ident[:])
                ins.then_inc(side_done, 1)

            def norm_transposes(what, n, h, k):
                pe.wait_ge(normed, TT * (n + 1))
                transposes(what, h, k, xn)

            def residual_transposes(h, k):
                pe.wait_ge(y_added, (h + 1) * TT * E1)
                transposes("x1t", h, k, x[:, h * TT:(h + 1) * TT])

            def layer_1(h, m):
                n = h * KC + m
                pe.wait_ge(xhi_done, (h + 1) * KC)
                pe.wait_ge(xlo_done, (h + 1) * KC)
                f = slice(m * P, (m + 1) * P)
                for e in range(E1):
                    if n == 0:
                        pe.wait_ge(w_hi, e + 1)
                        pe.wait_ge(w_lo, e + 1)
                    elif e == 0:
                        pe.wait_ge(z_first, n)
                    else:
                        pe.wait_ge(z_picked, (n - 1) * (E1 - 1) + e)
                    for k in range(KC):
                        ins = split_product(work[e][:], (ctx_hi[:, e, k, f], ctx_lo[:, e, k, f]),
                                            (xt_hi[:, h, k], xt_lo[:, h, k]), k == 0, k == KC - 1)
                    ins.then_inc(z_done, 1)

            def layer_2(h, t):
                T = h * TT + t
                pe.wait_ge(h1_done, (h + 1) * KC)
                if T >= 2:
                    pe.wait_ge(y_added, (T - 1) * E1)
                else:
                    pe.wait_ge(z_first, HALVES * KC)
                    pe.wait_ge(z_picked, HALVES * KC * (E1 - 1))
                s = slice(t * P, (t + 1) * P)
                for k in range(KC):
                    for a, b in ((0, 0), (0, 1), (1, 0)):
                        for pair in range(E1 // 2):
                            lhs = (h_hi, h_lo)[a][:, h, k, s]
                            rhs = (ctx_hi, ctx_lo)[b][:, 2 * pair:2 * pair + 2, k]
                            out = work[2 * (T % 2) + pair][:].rearrange("p (e d) -> p e d", e=2)
                            ins = nc.tensor.matmul(out, lhs, rhs,
                                                   start=(k == 0 and a == b), stop=(k == KC - 1 and a == 1))
                ins.then_inc(y_done, 1)

            def router(h):
                pe.wait_ge(xhi_done, (HALVES + h + 1) * KC)
                pe.wait_ge(xlo_done, (HALVES + h + 1) * KC)
                pe.wait_ge(rw_done, 1)
                b = side_wait("router", h, 0)
                for t in range(TT):
                    s = slice(t * P, (t + 1) * P)
                    for k in range(KC):
                        for n, (lhs, rhs) in enumerate(((xt_hi, rw_hi), (xt_hi, rw_lo), (xt_lo, rw_hi), (xt_lo, rw_lo))):
                            ins = nc.tensor.matmul(b[:, t * E2:(t + 1) * E2], lhs[:, h, k, s], rhs[:, k],
                                                   start=(k == 0 and n == 0), stop=(k == KC - 1 and n == 3))
                ins.then_inc(side_done, 1)

            def combine_transposes(h):
                pe.wait_ge(combined, h + 1)
                b = side_wait("combt", h, 0)
                for t in range(TT):
                    ins = nc.tensor.transpose(b[0:2 * E2, t * P:(t + 1) * P], comb2[:, t], ident[:])
                ins.then_inc(side_done, 1)

            def gate_up(g):
                h, c = items[g]
                w = widths(c)
                if c == 0:
                    pe.wait_ge(xhi_done, (HALVES + h + 1) * KC)
                    pe.wait_ge(xlo_done, (HALVES + h + 1) * KC)
                if h == 0:
                    n = gu_piece(c)
                    pe.wait_ge(w_hi, n + 1)
                    pe.wait_ge(w_lo, lows.index(n) + 1)
                for up in range(2):
                    if g < 2:
                        pe.wait_ge(y_added, HALVES * TT * E1)
                    elif up == 0:
                        pe.wait_ge(silu_done, g - 1)
                    else:
                        pe.wait_ge(prod_done, g - 1)
                    for k in range(KC):
                        cols = gu_cols(c, k, up)
                        ins = split_product(work[2 * (g % 2) + up][0:w, :], (gu_hi[:, cols], gu_lo[:, cols]),
                                            (xt_hi[:, h, k], xt_lo[:, h, k]), k == 0, k == KC - 1)
                    ins.then_inc(up_done if up else gate_done, 1)

            def combine_weights(g):
                h, c = items[g]
                if c == 0:
                    return
                if g == 1:
                    wait_side_read(pe, 4, len(side_order))
                    pe.wait_ge(w_hi, last_piece["sel"] + 1)
                pe.wait_ge(combt_done, h + 1)
                if g >= 2:
                    pe.wait_ge(hid_done, c_before(g - 1))
                nc.tensor.matmul(bank[4][:], sel_r[:, c - 1], combt[:, h], start=True, stop=True).then_inc(c_done, 1)

            def down(g):
                h, c = items[g]
                w = widths(c)
                if h == 0:
                    n = wd_piece(c)
                    pe.wait_ge(w_hi, n + 1)
                    pe.wait_ge(w_lo, lows.index(n) + 1)
                elif c == 0:
                    pe.wait_ge(out_ready, h * KC)
                pe.wait_ge(hlo_done, g + 1)
                r = ((g // 2) % 2, g % 2)
                for k in range(KC):
                    cols = slice(k * P, (k + 1) * P)
                    ins = split_product(acc[k][:], (wd_hi[0:w, c, cols], wd_lo[0:w, c, cols]),
                                        (h_hi[0:w, r[0], r[1]], h_lo[0:w, r[0], r[1]]), c == 0, c == ITEMS - 1)
                ins.then_inc(down_done, 1)

            pe.wait_ge(ident_in, 16)
            norm_transposes("n1", 0, 0, 0)
            norm_transposes("n1", 0, 0, 1)
            layer_1(0, 0)
            norm_transposes("n1", 1, 1, 0)
            norm_transposes("n1", 1, 1, 1)
            layer_1(0, 1)
            layer_1(1, 0)
            layer_1(1, 1)
            for t in range(TT):
                layer_2(0, t)
            layer_2(1, 0)
            residual_transposes(0, 0)
            residual_transposes(0, 1)
            layer_2(1, 1)
            norm_transposes("n2", 2, 0, 0)
            norm_transposes("n2", 2, 0, 1)
            layer_2(1, 2)
            layer_2(1, 3)
            router(0)
            for g in range(N + 2):
                if g < N:
                    gate_up(g)
                if g == 2:
                    combine_transposes(0)
                    norm_transposes("n2", 3, 1, 0)
                if g == 3:
                    norm_transposes("n2", 3, 1, 1)
                if g == 4:
                    residual_transposes(1, 0)
                if g == 5:
                    residual_transposes(1, 1)
                if g == 7:
                    router(1)
                if g == 11:
                    combine_transposes(1)
                if 1 <= g <= N:
                    combine_weights(g - 1)
                if g >= 2:
                    down(g - 2)


def kernel(**inputs):
    import numpy as np
    import concourse.bacc as bacc
    from concourse.bass_utils import run_bass_kernel_spmd

    a = {k: np.asarray(v) for k, v in inputs.items()}
    gup, dp = a["L0_ffn_gate_up_proj"], a["L0_ffn_down_proj"]
    gate = gup[:, :I, :].reshape(E2 * I, D)
    up = gup[:, I:, :].reshape(E2 * I, D)

    def feature_major(*mats):
        return np.stack([m.T.reshape(KC, P, m.shape[0]).transpose(1, 0, 2) for m in mats], axis=2)

    shared = feature_major(a["L0_ffn_shared_gate_w"], a["L0_ffn_shared_up_w"]).reshape(P, SH)
    routed = feature_major(gate, up).reshape(P, KC, 2, CH, P).transpose(0, 3, 1, 2, 4).reshape(P, CH * CW)
    ids = a["itok_BxS_13_99985"].reshape(TOKENS)
    sel = np.zeros((2, E2, CH * P), np.float32)
    sel[:, np.arange(CH * P) // I, np.arange(CH * P)] = 1.0
    arrays = {
        "x_d": a["x"].reshape(HALVES * TT, P, D).transpose(1, 0, 2),
        "idrow_d": ids,
        "idcol_d": ids.reshape(HALVES * TT, P).T,
        "ctx_d": a["ctx_2048"].transpose(2, 0, 1).reshape(KC, P, E1, D).transpose(1, 2, 0, 3),
        "rw_d": a["L0_ffn_router_w"].T.reshape(KC, P, E2).transpose(1, 0, 2),
        "bias_d": a["L0_ffn_e_bias"],
        "gu_d": np.concatenate([shared, routed], axis=1),
        "wd0_d": a["L0_ffn_shared_down_w"].T,
        "wd_d": dp.transpose(0, 2, 1).reshape(CH, P, D).transpose(1, 0, 2).reshape(P, CH * D),
        "sel_d": sel.reshape(2 * E2, CH * P),
        "ident_d": np.eye(P, dtype=np.float32),
    }
    arrays = {k: np.ascontiguousarray(v) for k, v in arrays.items()}
    nc = bacc.Bacc("TRN2", target_bir_lowering=False, num_devices=1)
    aps = [nc.dram_tensor(k, v.shape, mybir.dt.from_np(v.dtype), kind="ExternalInput").ap() for k, v in arrays.items()]
    out = nc.dram_tensor("out_d", (P, KC, TOKENS), F32, kind="ExternalOutput").ap()
    build(nc, *aps, out)
    r = run_bass_kernel_spmd(nc, [arrays], core_ids=[0])
    got = r.results[0]["out_d"]
    return np.ascontiguousarray(got.transpose(1, 0, 2).reshape(D, TOKENS).T).reshape(a["x"].shape)
```

```python
from contextlib import ExitStack

import concourse.bass as bass
from concourse import mybir

F32 = mybir.dt.float32
F32R = mybir.dt.float32r
I32 = mybir.dt.int32
U8 = mybir.dt.uint8
BF16 = mybir.dt.bfloat16
ALU = mybir.AluOpType
ACT = mybir.ActivationFunctionType
AX = mybir.AxisListType

P = 128
TOKENS = 1024
D = 256
KC = D // P
HALF = 512
HALVES = TOKENS // HALF
TT = HALF // P
E1 = 4
VOCAB = 12500
PER_EXPERT = VOCAB // E1
EPS = 1e-5

E2 = 16
TOP = 4
I = 96
CH = E2 * I // P
ITEMS = CH + 1
RW = I
SHK = P + I
SH = KC * SHK
CW = 2 * KC * P
GU = SH + CH * CW
WARM_UP = 20
SENTINEL = -3.0e38
MARK = 3.0e38

STAGE = 1024
SLOTS = 4
RING = HALVES * KC


def weight_pieces():
    pieces = [("ctx", e * KC * D, KC * D) for e in range(E1)]
    pieces += [("gu", 0, SH)] + [("gu", c, STAGE) for c in range(SH, GU, STAGE)]
    pieces += [("sel", c, CH * P // 2) for c in (0, CH * P // 2)]
    pieces += [("wd0", 0, D)] + [("wd", c, STAGE) for c in range(0, CH * D, STAGE)]
    return pieces


def build(nc, x_d, idrow_d, idcol_d, ctx_d, bias_d, gu_d, wd0_d, wd_d, sel_d, consts_d, out_d):
    pieces = weight_pieces()
    last_piece = {what: n for n, (what, _, _) in enumerate(pieces)}
    lows = [n for n, (what, _, _) in enumerate(pieces) if what != "sel"]

    with ExitStack() as ctx:
        def sb(name, shape, dt=F32):
            return ctx.enter_context(nc.sbuf_tensor(name, shape, dt))

        def sem(name):
            return ctx.enter_context(nc.semaphore(name))

        x = sb("x", [P, HALVES * TT, D])
        x1t = sb("x1t", [P, KC, TOKENS])
        stage = sb("stage", [P, SLOTS, STAGE])
        ctx_hi = sb("ctx_hi", [P, E1, KC, D], F32R)
        ctx_lo = sb("ctx_lo", [P, E1, KC, D], F32R)
        gu_hi = sb("gu_hi", [P, GU], F32R)
        gu_lo = sb("gu_lo", [P, GU], F32R)
        wd_hi = sb("wd_hi", [P, ITEMS, D], F32R)
        wd_lo = sb("wd_lo", [P, ITEMS, D], F32R)
        sel_r = sb("sel_r", [2 * E2, CH, P], F32R)
        consts_sb = sb("consts_sb", [P, P + E2])
        warm = sb("warm", [P, HALF], BF16)
        idrow = sb("idrow", [P, TOKENS], I32)
        idcol = sb("idcol", [P, HALVES * TT], I32)
        gerow = sb("gerow", [P, E1 - 1, TOKENS], U8)
        gecol = sb("gecol", [P, E1 + 1, HALVES * TT])
        pick = sb("pick", [P, E1, HALVES * TT])
        stats = sb("stats", [P, TT, 6])
        meanvar = sb("meanvar", [P, TT, 2])
        vareps = sb("vareps", [P, TT])
        rstd = sb("rstd", [P, TT])
        power = sb("power", [P, TT])
        xn = sb("xn", [P, TT, D])
        xt_hi = sb("xt_hi", [P, HALVES, KC, HALF], F32R)
        xt_lo = sb("xt_lo", [P, HALVES, KC, HALF], F32R)
        act_sb = sb("act_sb", [P, 2, HALF])
        prod = sb("prod", [P, 2, HALF])
        hid = sb("hid", [P, 2, HALF])
        h_hi = sb("h_hi", [P, RING + 1, HALF], F32R)
        h_lo = sb("h_lo", [P, RING + 1, HALF], F32R)
        logits = sb("logits", [P, HALF])
        bias = sb("bias", [P, E2])
        scores = sb("scores", [P, TT, E2])
        biased = sb("biased", [P, TT, E2 + 4])
        best = sb("best", [P, TT, 8])
        marked = sb("marked", [P, TT, E2 + 4])
        weight = sb("weight", [P, TT, E2])
        wsum = sb("wsum", [P, TT])
        wsume = sb("wsume", [P, TT])
        winv = sb("winv", [P, TT])
        comb = sb("comb", [P, TT, E2])
        comb2 = sb("comb2", [P, TT, 2 * E2])
        combt = sb("combt", [2 * E2, HALVES, HALF], F32R)

        bank = [ctx.enter_context(nc.psum_tensor(f"bank{n}", [P, HALF], F32)) for n in range(8)]
        work = bank[0:4]
        side = bank[4:6]
        acc = bank[6:8]

        x_in = [sem(f"x_in{n}") for n in range(3)]
        slot_in = [sem(f"slot_in{s}") for s in range(SLOTS)]
        idrow_in, idcol_in, bias_in, ident_in = sem("idrow_in"), sem("idcol_in"), sem("bias_in"), sem("ident_in")
        out_written = sem("out_written")
        w_hi, w_lo = sem("w_hi"), sem("w_lo")
        consts, warm_set = sem("consts"), sem("warm_set")
        dstep = sem("dstep")
        varied, powered, normed = sem("varied"), sem("powered"), sem("normed")
        side_done = sem("side_done")
        xhi_done, xlo_done = sem("xhi_done"), sem("xlo_done")
        z_done, z_first, z_silu, h1_done = sem("z_done"), sem("z_first"), sem("z_silu"), sem("h1_done")
        z_picked = sem("z_picked")
        y_done, y_added = sem("y_done"), sem("y_added")
        rw_done, logits_done, scored, combined, combt_done = sem("rw_done"), sem("logits_done"), sem("scored"), sem("combined"), sem("combt_done")
        gate_done, up_done, silu_done, prod_done = sem("gate_done"), sem("up_done"), sem("silu_done"), sem("prod_done")
        c_done, hid_done, hhi_done, hlo_done, down_done = sem("c_done"), sem("hid_done"), sem("hhi_done"), sem("hlo_done"), sem("down_done")
        x1t_done, acc_done, out_ready = sem("x1t_done"), sem("acc_done"), sem("out_ready")

        side_order = [("n1", 0, 0, 4), ("n1", 0, 1, 5), ("n1", 1, 0, 4), ("n1", 1, 1, 5),
                      ("x1t", 0, 0, 4), ("x1t", 0, 1, 5), ("n2", 0, 0, 4), ("n2", 0, 1, 5),
                      ("router", 0, 0, 5), ("combt", 0, 0, 5),
                      ("n2", 1, 0, 5), ("n2", 1, 1, 5), ("x1t", 1, 0, 5), ("x1t", 1, 1, 5),
                      ("router", 1, 0, 5), ("combt", 1, 0, 5)]
        side_at = {u[:3]: n for n, u in enumerate(side_order)}

        def wait_side_read(eng, b, n):
            before = [u for u in side_order[:n] if u[3] == b]
            if not before:
                return
            what, h, k, _ = before[-1]
            if what in ("n1", "n2"):
                count = (HALVES * KC if what == "n2" else 0) + h * KC + k + 1
                eng.wait_ge(xhi_done, count)
                eng.wait_ge(xlo_done, count)
            elif what == "x1t":
                eng.wait_ge(x1t_done, h * KC + k + 1)
            elif what == "router":
                eng.wait_ge(scored, h + 1)
            else:
                eng.wait_ge(combt_done, h + 1)

        def side_bank(what, h, c):
            return bank[side_order[side_at[what, h, c]][3]]

        def widths(c):
            return I if c == 0 else P

        def gu_cols(c, k, up):
            if c == 0:
                at = k * SHK + up * P
                return slice(at, at + I)
            at = SH + (c - 1) * CW + (k * 2 + up) * P
            return slice(at, at + P)

        def gu_piece(c):
            return last_piece["ctx"] + 1 + (0 if c == 0 else 1 + (c - 1) * CW // STAGE)

        def wd_piece(c):
            return last_piece["wd0"] + (0 if c == 0 else 1 + (c - 1) * D // STAGE)

        early = 8
        items = [(0, c) for c in range(early + 1)] + [(1, 0)]
        items += [(0, c) for c in range(early + 1, ITEMS)] + [(1, c) for c in range(1, ITEMS)]
        N = len(items)
        place = {item: g for g, item in enumerate(items)}
        downs = [place[h, c] for h in range(HALVES) for c in range(ITEMS)]
        ring = [g for g in range(N) if g != place[1, 0]]
        slot = {g: n % RING for n, g in enumerate(ring)} | {place[1, 0]: RING}
        former = {g: ring[n - RING] for n, g in enumerate(ring) if n >= RING}

        def routed(g):
            return sum(c > 0 for _, c in items[:g + 1])

        def wait_down(eng, g):
            h, c = items[g]
            if c == ITEMS - 1:
                eng.wait_ge(acc_done, (h + 1) * KC)
            else:
                eng.wait_ge(down_done, downs.index(g) + 1 - h)

        def gate_bank(g):
            return acc[0] if g == 0 else work[2 * ((g + 1) % 2)]

        def up_bank(g):
            return acc[1] if g == 0 else work[2 * ((g + 1) % 2) + 1]

        def piece_aps(n):
            what, at, cols = pieces[n]
            st = stage[:, n % SLOTS, 0:cols]
            if what == "ctx":
                e = at // (KC * D)
                st = st.rearrange("p (k f) -> p k f", k=KC)
                return ctx_d[:, e], st, ctx_hi[:, e], ctx_lo[:, e]
            if what == "gu":
                return gu_d[:, at:at + cols], st, gu_hi[:, at:at + cols], gu_lo[:, at:at + cols]
            if what == "sel":
                st = stage[0:2 * E2, n % SLOTS, 0:cols]
                hi = sel_r[:, :, :].rearrange("k c r -> k (c r)")[:, at:at + cols]
                return sel_d[:, at:at + cols], st, hi, None
            if what == "wd0":
                st = stage[0:I, n % SLOTS, 0:cols]
                return wd0_d, st, wd_hi[0:I, 0], wd_lo[0:I, 0]
            hi = wd_hi[:, 1:, :].rearrange("p c d -> p (c d)")[:, at:at + cols]
            lo = wd_lo[:, 1:, :].rearrange("p c d -> p (c d)")[:, at:at + cols]
            return wd_d[:, at:at + cols], st, hi, lo

        block = ctx.enter_context(nc.Block())

        @block.sync
        def _(sp):
            def load_piece(n):
                if n >= SLOTS:
                    sp.wait_ge(w_hi, n - SLOTS + 1)
                    before = sum(m <= n - SLOTS for m in lows)
                    sp.wait_ge(w_lo, before)
                dram, st, _, _ = piece_aps(n)
                sp.dma_start(st, dram).then_inc(slot_in[n % SLOTS], 16)

            sp.dma_start(x[:, 0:TT // 2], x_d[:, 0:TT // 2]).then_inc(x_in[0], 16)
            sp.dma_start(x[:, TT // 2:TT], x_d[:, TT // 2:TT]).then_inc(x_in[1], 16)
            load_piece(0)
            sp.dma_start(consts_sb[:], consts_d).then_inc(ident_in, 16)
            load_piece(1)
            sp.dma_start(idrow[:], idrow_d.partition_broadcast(P)).then_inc(idrow_in, 16)
            load_piece(2)
            sp.dma_start(x[:, TT:], x_d[:, TT:]).then_inc(x_in[2], 16)
            load_piece(3)
            sp.dma_start(idcol[:], idcol_d).then_inc(idcol_in, 16)
            sp.dma_start(bias[:], bias_d.partition_broadcast(P)).then_inc(bias_in, 16)
            for n in range(4, len(pieces)):
                load_piece(n)
            for h in range(HALVES):
                for k in range(KC):
                    sp.wait_ge(out_ready, h * KC + k + 1)
                    sp.dma_start(out_d[:, k, h * HALF:(h + 1) * HALF],
                                 x1t[:, k, h * HALF:(h + 1) * HALF]).then_inc(out_written, 16)
            sp.wait_ge(out_written, 16 * HALVES * KC)

        @block.gpsimd
        def _(pool):
            nc.gpsimd.memset(warm[:], 0.0).then_inc(warm_set, 1)
            nc.gpsimd.memset(power[:], -0.5).then_inc(consts, 1)
            nc.gpsimd.memset(biased[:, :, E2:], SENTINEL).then_inc(consts, 1)
            pool.wait_ge(consts, 2)

            def low_part(n):
                pool.wait_ge(w_hi, n + 1)
                pool.wait_ge(slot_in[n % SLOTS], 16 * (n // SLOTS + 1))
                _, st, hi, lo = piece_aps(n)
                nc.gpsimd.tensor_tensor(lo, st, hi.bitcast(F32), ALU.subtract).then_inc(w_lo, 1)

            def rstd_of(n, cols=slice(0, TT)):
                pool.wait_ge(varied, n + 1)
                if n >= 2:
                    pool.wait_ge(normed, TT * (n - 1))
                nc.gpsimd.tensor_tensor(rstd[:, cols], vareps[:, cols], power[:, cols], ALU.pow).then_inc(powered, 1)

            rstd_of(0, slice(0, TT // 2))
            rstd_of(1, slice(TT // 2, TT))
            for n in range(E1):
                low_part(n)
            rstd_of(2)
            for n in lows[E1:]:
                low_part(n)
            rstd_of(3)
            rstd_of(4)

        @block.scalar
        def _(act):
            def high_part(n):
                act.wait_ge(slot_in[n % SLOTS], 16 * (n // SLOTS + 1))
                _, st, hi, _ = piece_aps(n)
                nc.scalar.activation(hi, st, ACT.Copy).then_inc(w_hi, 1)

            def x_high(what, h, k):
                act.wait_ge(side_done, side_at[what, h, k] + 1)
                if what == "n2":
                    act.wait_ge(z_done, (h + 1) * KC * E1)
                nc.scalar.activation(xt_hi[:, h, k], side_bank(what, h, k)[:], ACT.Copy).then_inc(xhi_done, 1)

            def first_z(h, m):
                n = h * KC + m
                act.wait_ge(z_done, n * E1 + 1)
                if n >= 2:
                    act.wait_ge(h1_done, n - 1)
                nc.scalar.activation(prod[:, n % 2], work[0][:], ACT.Copy).then_inc(z_first, 1)

            def silu_z(h, m):
                n = h * KC + m
                act.wait_ge(z_picked, (n + 1) * (E1 - 1))
                if n >= 2:
                    act.wait_ge(h1_done, n - 1)
                nc.scalar.activation(act_sb[:, n % 2], prod[:, n % 2], ACT.Silu).then_inc(z_silu, 1)

            def residual(h, k):
                u = side_at["x1t", h, k]
                act.wait_ge(side_done, u + 1)
                nc.scalar.activation(x1t[:, k, h * HALF:(h + 1) * HALF], side_bank("x1t", h, k)[:],
                                     ACT.Copy).then_inc(x1t_done, 1)

            def score(h):
                act.wait_ge(side_done, side_at["router", h, 0] + 1)
                if h:
                    act.wait_ge(combined, h)
                nc.scalar.activation(scores[:].rearrange("p t e -> p (t e)"),
                                     side_bank("router", h, 0)[:, 0:TT * E2], ACT.Sigmoid).then_inc(scored, 1)

            def combine_rows(h):
                act.wait_ge(side_done, side_at["combt", h, 0] + 1)
                nc.scalar.activation(combt[:, h], side_bank("combt", h, 0)[0:2 * E2, :], ACT.Copy).then_inc(combt_done, 1)

            def router_logits(h):
                act.wait_ge(gate_done, place[h, 0] + 1)
                if h:
                    act.wait_ge(side_done, side_at["router", h - 1, 0] + 1)
                nc.scalar.activation(logits[RW:, :], gate_bank(place[h, 0])[RW:, :], ACT.Copy).then_inc(logits_done, 1)

            def silu_gate(g):
                w = widths(items[g][1])
                act.wait_ge(gate_done, g + 1)
                if g >= 2:
                    act.wait_ge(hid_done, g - 1)
                else:
                    act.wait_ge(h1_done, HALVES * KC)
                nc.scalar.activation(act_sb[0:w, g % 2], gate_bank(g)[0:w, :], ACT.Silu).then_inc(silu_done, 1)

            def hid_high(g):
                w = widths(items[g][1])
                act.wait_ge(hid_done, g + 1)
                if g in former:
                    wait_down(act, former[g])
                elif g < RING:
                    act.wait_ge(y_done, TT if g < KC else HALVES * TT)
                nc.scalar.activation(h_hi[0:w, slot[g]], hid[0:w, g % 2], ACT.Copy).then_inc(hhi_done, 1)

            nc.scalar.preload_act_table(ACT.Silu)
            high_part(0)
            high_part(1)
            x_high("n1", 0, 0)
            x_high("n1", 0, 1)
            high_part(2)
            high_part(3)
            first_z(0, 0)
            x_high("n1", 1, 0)
            x_high("n1", 1, 1)
            silu_z(0, 0)
            high_part(4)
            high_part(5)
            first_z(0, 1)
            silu_z(0, 1)
            high_part(6)
            high_part(7)
            first_z(1, 0)
            silu_z(1, 0)
            high_part(8)
            high_part(9)
            first_z(1, 1)
            silu_z(1, 1)
            for n in range(10, len(pieces)):
                high_part(n)
            residual(0, 0)
            residual(0, 1)
            x_high("n2", 0, 0)
            x_high("n2", 0, 1)
            router_logits(0)
            silu_gate(0)
            score(0)
            hid_high(0)
            for g in range(1, N):
                if g == 3:
                    x_high("n2", 1, 0)
                if g == 4:
                    x_high("n2", 1, 1)
                if g == 5:
                    residual(1, 0)
                if g == 6:
                    residual(1, 1)
                if g == place[1, 0] + 2:
                    score(1)
                if g == place[1, 1]:
                    combine_rows(1)
                if g == place[1, 0]:
                    router_logits(1)
                silu_gate(g)
                if g == 1:
                    combine_rows(0)
                hid_high(g)

        @block.vector
        def _(dve):
            steps = [0]

            def step(ins):
                steps[0] += 1
                ins.then_inc(dstep, 1)
                return steps[0]

            def tile_stats(h, t):
                step(nc.vector.bn_stats(stats[:, t], x[:, h * TT + t]))

            def layer_norm_vars(tiles=range(TT)):
                dve.wait_ge(dstep, steps[0])
                for t in tiles:
                    step(nc.vector.bn_aggr(meanvar[:, t], stats[:, t]))
                dve.wait_ge(dstep, steps[0])
                s = slice(tiles[0], tiles[-1] + 1)
                nc.vector.tensor_scalar(vareps[:, s], meanvar[:, s, 1], EPS, None, ALU.add).then_inc(varied, 1)

            def layer_norm_apply(n, h, tiles=range(TT)):
                dve.wait_ge(powered, n + 1)
                if n > 1:
                    what, hh = [("n1", 0), ("n1", 1), ("n2", 0)][n - 2]
                    dve.wait_ge(side_done, side_at[what, hh, 1] + 1)
                for t in tiles:
                    nc.vector.tensor_scalar(xn[:, t], x[:, h * TT + t], meanvar[:, t, 0:1], rstd[:, t:t + 1],
                                            ALU.subtract, ALU.mult).then_inc(normed, 1)

            def x_low(what, h, k):
                n = (HALVES * KC if what == "n2" else 0) + h * KC + k
                dve.wait_ge(xhi_done, n + 1)
                dve.wait_ge(side_done, side_at[what, h, k] + 1)
                nc.vector.tensor_tensor(xt_lo[:, h, k], side_bank(what, h, k)[:], xt_hi[:, h, k].bitcast(F32),
                                        ALU.subtract).then_inc(xlo_done, 1)

            def masks_row(h):
                if h == 0:
                    dve.wait_ge(idrow_in, 16)
                for e in range(1, E1):
                    last = step(nc.vector.tensor_scalar(gerow[:, e - 1, h * HALF:(h + 1) * HALF],
                                                        idrow[:, h * HALF:(h + 1) * HALF],
                                                        float(e * PER_EXPERT), None, ALU.is_ge))
                return last

            def masks_col():
                dve.wait_ge(idcol_in, 16)
                step(nc.vector.memset(gecol[:, 0], 1.0))
                step(nc.vector.memset(gecol[:, E1], 0.0))
                for e in range(1, E1):
                    step(nc.vector.tensor_scalar(gecol[:, e], idcol[:], float(e * PER_EXPERT), None, ALU.is_ge))
                dve.wait_ge(dstep, steps[0])
                return step(nc.vector.tensor_tensor(pick[:], gecol[:, 0:E1], gecol[:, 1:], ALU.subtract))

            def pick_z(h, m, masked):
                n = h * KC + m
                dve.wait_ge(z_first, n + 1)
                dve.wait_ge(dstep, masked)
                for e in range(1, E1):
                    dve.wait_ge(z_done, n * E1 + e + 1)
                    if e > 1:
                        dve.wait_ge(z_picked, n * (E1 - 1) + e - 1)
                    ins = nc.vector.copy_predicated(prod[:, n % 2], gerow[:, e - 1, h * HALF:(h + 1) * HALF], work[e][:])
                    ins.then_inc(z_picked, 1)

            def hidden_1(h, m):
                n = h * KC + m
                dve.wait_ge(z_silu, n + 1)
                last = step(nc.vector.tensor_tensor(hid[:, n % 2], act_sb[:, n % 2], prod[:, n % 2], ALU.mult))
                dve.wait_ge(dstep, last)
                last = step(nc.vector.tensor_scalar(h_hi[:, h * KC + m], hid[:, n % 2], 1.0, None, ALU.mult))
                dve.wait_ge(dstep, last)
                nc.vector.tensor_tensor(h_lo[:, h * KC + m], hid[:, n % 2], h_hi[:, h * KC + m].bitcast(F32),
                                        ALU.subtract).then_inc(h1_done, 1)

            def add_y(h, t, picked):
                T = h * TT + t
                dve.wait_ge(y_done, T + 1)
                dve.wait_ge(dstep, picked)
                for e in range(E1):
                    y = work[2 * (T % 2) + e // 2][:, (e % 2) * D:(e % 2 + 1) * D]
                    ins = nc.vector.scalar_tensor_tensor(out=x[:, T], in0=y, scalar=pick[:, e, T:T + 1],
                                                         in1=x[:, T], op0=ALU.mult, op1=ALU.add)
                    ins.then_inc(y_added, 1)
                    dve.wait_ge(y_added, T * E1 + e + 1)
                tile_stats(h, t)

            def router_low_rows():
                n = gu_piece(0)
                dve.wait_ge(w_hi, n + 1)
                dve.wait_ge(w_lo, lows.index(n) + 1)
                hi, lo = (w[:, 0:SH].rearrange("p (k c) -> p k c", k=KC) for w in (gu_hi, gu_lo))
                nc.vector.tensor_copy(hi[:, :, RW + E2:RW + 2 * E2], lo[:, :, RW:RW + E2].bitcast(F32)).then_inc(rw_done, 1)

            def route(h):
                dve.wait_ge(scored, h + 1)
                dve.wait_ge(consts, 2)
                dve.wait_ge(bias_in, 16)
                if h:
                    dve.wait_ge(side_done, side_at["combt", h - 1, 0] + 1)
                last = step(nc.vector.tensor_tensor(
                    biased[:, :, 0:E2], scores[:], bias[:].unsqueeze(1).to_broadcast([P, TT, E2]), ALU.add))
                dve.wait_ge(dstep, last)
                for t in range(TT):
                    last = step(nc.vector.max(best[:, t], biased[:, t, 0:E2]))
                dve.wait_ge(dstep, last)
                last = step(nc.vector.memset(best[:, :, TOP:], SENTINEL))
                dve.wait_ge(dstep, last)
                for t in range(TT):
                    last = step(nc.vector.match_replace(marked[:, t], best[:, t], biased[:, t], MARK))
                dve.wait_ge(dstep, last)
                last = step(nc.vector.scalar_tensor_tensor(out=weight[:], in0=marked[:, :, 0:E2], scalar=MARK, in1=scores[:],
                                                           op0=ALU.is_equal, op1=ALU.mult))
                dve.wait_ge(dstep, last)
                last = step(nc.vector.tensor_reduce(wsum[:], weight[:], AX.X, ALU.add))
                dve.wait_ge(dstep, last)
                last = step(nc.vector.tensor_scalar(wsume[:], wsum[:], 1e-20, None, ALU.add))
                dve.wait_ge(dstep, last)
                last = step(nc.vector.reciprocal(winv[:], wsume[:]))
                dve.wait_ge(dstep, last)
                last = step(nc.vector.tensor_tensor(comb[:], weight[:], winv[:].unsqueeze(2).to_broadcast([P, TT, E2]), ALU.mult))
                dve.wait_ge(dstep, last)
                last = step(nc.vector.tensor_scalar(comb2[:, :, 0:E2].bitcast(F32R), comb[:], 1.0, None, ALU.mult))
                dve.wait_ge(dstep, last)
                nc.vector.tensor_tensor(comb2[:, :, E2:], comb[:], comb2[:, :, 0:E2], ALU.subtract).then_inc(combined, 1)

            def product(g):
                if items[g][1] == 0:
                    return
                dve.wait_ge(silu_done, g + 1)
                dve.wait_ge(c_done, routed(g))
                nc.vector.tensor_tensor(prod[:, g % 2], act_sb[:, g % 2], bank[4][:], ALU.mult).then_inc(prod_done, 1)

            def hidden_2(g):
                w = widths(items[g][1])
                if items[g][1] == 0:
                    dve.wait_ge(silu_done, g + 1)
                else:
                    dve.wait_ge(prod_done, routed(g))
                dve.wait_ge(up_done, g + 1)
                if g >= 2:
                    dve.wait_ge(hhi_done, g - 1)
                src = (act_sb if items[g][1] == 0 else prod)[0:w, g % 2]
                nc.vector.tensor_tensor(hid[0:w, g % 2], src, up_bank(g)[0:w, :], ALU.mult).then_inc(hid_done, 1)

            def hid_low(g):
                w = widths(items[g][1])
                dve.wait_ge(hhi_done, g + 1)
                nc.vector.tensor_tensor(h_lo[0:w, slot[g]], hid[0:w, g % 2], h_hi[0:w, slot[g]].bitcast(F32),
                                        ALU.subtract).then_inc(hlo_done, 1)

            def output(h):
                dve.wait_ge(x1t_done, (h + 1) * KC)
                for k in range(KC):
                    dve.wait_ge(acc_done, h * KC + k + 1)
                    o = x1t[:, k, h * HALF:(h + 1) * HALF]
                    nc.vector.tensor_tensor(o, acc[k][:], o, ALU.add).then_inc(out_ready, 1)

            for n, tiles in enumerate((range(TT // 2), range(TT // 2, TT))):
                dve.wait_ge(x_in[n], 16)
                for t in tiles:
                    tile_stats(0, t)
                layer_norm_vars(tiles)
            for n, tiles in enumerate((range(TT // 2), range(TT // 2, TT))):
                layer_norm_apply(n, 0, tiles)
            dve.wait_ge(x_in[2], 16)
            for t in range(TT):
                tile_stats(1, t)
            x_low("n1", 0, 0)
            x_low("n1", 0, 1)
            layer_norm_vars()
            masked = masks_row(0)
            layer_norm_apply(2, 1)
            pick_z(0, 0, masked)
            x_low("n1", 1, 0)
            x_low("n1", 1, 1)
            hidden_1(0, 0)
            masked = masks_row(1)
            pick_z(0, 1, masked)
            hidden_1(0, 1)
            picked = masks_col()
            router_low_rows()
            for m in range(KC):
                pick_z(1, m, masked)
                hidden_1(1, m)
            for t in range(TT):
                add_y(0, t, picked)
            layer_norm_vars()
            layer_norm_apply(3, 0)
            add_y(1, 0, picked)
            add_y(1, 1, picked)
            x_low("n2", 0, 0)
            x_low("n2", 0, 1)
            add_y(1, 2, picked)
            hidden_2(0)
            hid_low(0)
            route(0)
            add_y(1, 3, picked)
            layer_norm_vars()
            product(1)
            hidden_2(1)
            layer_norm_apply(4, 1)
            hid_low(1)
            for g in range(2, N):
                if g == 3:
                    x_low("n2", 1, 0)
                if g == 4:
                    x_low("n2", 1, 1)
                if g == place[1, 1] + 1:
                    output(0)
                product(g)
                hidden_2(g)
                hid_low(g)
                if g == place[1, 0] + 2:
                    route(1)
            output(1)

        @block.tensor
        def _(pe):
            def side_wait(what, h, c):
                u = side_at[what, h, c]
                b = side_order[u][3]
                wait_side_read(pe, b, u)
                return bank[b]

            def split_product(out, lhs, rhs, first, last):
                for n, (a, b) in enumerate(((0, 0), (0, 1), (1, 0))):
                    ins = nc.tensor.matmul(out, lhs[a], rhs[b], start=(first and n == 0), stop=(last and n == 2))
                return ins

            def transposes(what, h, k, src):
                b = side_wait(what, h, k)
                for t in range(TT):
                    ins = nc.tensor.transpose(b[:, t * P:(t + 1) * P], src[:, t, k * P:(k + 1) * P], consts_sb[:, 0:P])
                ins.then_inc(side_done, 1)

            def norm_transposes(what, n, h, k):
                pe.wait_ge(normed, TT * (n + 1))
                transposes(what, h, k, xn)

            def residual_transposes(h, k):
                pe.wait_ge(y_added, (h + 1) * TT * E1)
                transposes("x1t", h, k, x[:, h * TT:(h + 1) * TT])

            def layer_1(h, m):
                n = h * KC + m
                f = slice(m * P, (m + 1) * P)
                for e in range(E1):
                    if n == 0:
                        pe.wait_ge(w_hi, e + 1)
                        pe.wait_ge(w_lo, e + 1)
                    elif e == 0:
                        pe.wait_ge(z_first, n)
                    else:
                        pe.wait_ge(z_picked, (n - 1) * (E1 - 1) + e)
                    for w, xt, xt_done in ((ctx_hi, xt_hi, xhi_done), (ctx_lo, xt_hi, xhi_done), (ctx_hi, xt_lo, xlo_done)):
                        for k in range(KC):
                            if e == m == 0:
                                pe.wait_ge(xt_done, h * KC + k + 1)
                            ins = nc.tensor.matmul(work[e][:], w[:, e, k, f], xt[:, h, k],
                                                   start=(w is ctx_hi and xt is xt_hi and k == 0),
                                                   stop=(xt is xt_lo and k == KC - 1))
                    ins.then_inc(z_done, 1)

            def layer_2(h, t):
                T = h * TT + t
                pe.wait_ge(h1_done, (h + 1) * KC)
                if T >= 2:
                    pe.wait_ge(y_added, (T - 1) * E1)
                else:
                    pe.wait_ge(z_first, HALVES * KC)
                    pe.wait_ge(z_picked, HALVES * KC * (E1 - 1) - 2 * (1 - T))
                s = slice(t * P, (t + 1) * P)
                for k in range(KC):
                    for a, b in ((0, 0), (0, 1), (1, 0)):
                        for pair in range(E1 // 2):
                            lhs = (h_hi, h_lo)[a][:, h * KC + k, s]
                            rhs = (ctx_hi, ctx_lo)[b][:, 2 * pair:2 * pair + 2, k]
                            out = work[2 * (T % 2) + pair][:].rearrange("p (e d) -> p e d", e=2)
                            ins = nc.tensor.matmul(out, lhs, rhs,
                                                   start=(k == 0 and a == b), stop=(k == KC - 1 and a == 1))
                ins.then_inc(y_done, 1)

            def router(h):
                pe.wait_ge(logits_done, h + 1)
                b = side_wait("router", h, 0)
                for t in range(TT):
                    ins = nc.tensor.matmul(b[:, t * E2:(t + 1) * E2], logits[RW:, t * P:(t + 1) * P],
                                           consts_sb[RW:, P:], start=True, stop=True)
                ins.then_inc(side_done, 1)

            def combine_transposes(h):
                pe.wait_ge(combined, h + 1)
                b = side_wait("combt", h, 0)
                for t in range(TT):
                    ins = nc.tensor.transpose(b[0:2 * E2, t * P:(t + 1) * P], comb2[:, t], consts_sb[:, 0:P])
                ins.then_inc(side_done, 1)

            def gate_or_up(g, up):
                h, c = items[g]
                w = widths(c)
                if h == 0:
                    n = gu_piece(c)
                    pe.wait_ge(w_hi, n + 1)
                    pe.wait_ge(w_lo, lows.index(n) + 1)
                if c == 0:
                    pe.wait_ge(rw_done, 1)
                    pe.wait_ge(xhi_done, (HALVES + h + 1) * KC)
                    pe.wait_ge(xlo_done, (HALVES + h + 1) * KC)
                if g == 1 or g == 2:
                    pe.wait_ge(y_added, (HALVES * TT - 2 + g) * E1)
                elif g > 2 and up:
                    pe.wait_ge(hid_done, g - 1)
                elif g > 2:
                    pe.wait_ge(silu_done, g - 1)
                    if items[g - 2][1] == 0:
                        pe.wait_ge(logits_done, items[g - 2][0] + 1)
                out = (up_bank if up else gate_bank)(g)
                for k in range(KC):
                    cols = gu_cols(c, k, up)
                    wide = slice(cols.start, cols.start + P) if c == 0 and not up else cols
                    rows = wide.stop - wide.start
                    nc.tensor.matmul(out[0:rows, :], gu_hi[:, wide], xt_hi[:, h, k], start=(k == 0), stop=False)
                    nc.tensor.matmul(out[0:w, :], gu_lo[:, cols], xt_hi[:, h, k], start=False, stop=False)
                    ins = nc.tensor.matmul(out[0:rows, :], gu_hi[:, wide], xt_lo[:, h, k], start=False, stop=(k == KC - 1))
                ins.then_inc(up_done if up else gate_done, 1)

            def combine_weights(g):
                h, c = items[g]
                if c == 0:
                    return
                if routed(g) == 1:
                    wait_side_read(pe, 4, len(side_order))
                    pe.wait_ge(w_hi, last_piece["sel"] + 1)
                else:
                    pe.wait_ge(prod_done, routed(g) - 1)
                pe.wait_ge(combt_done, h + 1)
                nc.tensor.matmul(bank[4][:], sel_r[:, c - 1], combt[:, h], start=True, stop=True).then_inc(c_done, 1)

            def down(g):
                h, c = items[g]
                w = widths(c)
                if h == 0:
                    n = wd_piece(c)
                    pe.wait_ge(w_hi, n + 1)
                    pe.wait_ge(w_lo, lows.index(n) + 1)
                if g == 0:
                    pe.wait_ge(logits_done, 1)
                elif c == 0:
                    pe.wait_ge(out_ready, h * KC)
                pe.wait_ge(hlo_done, g + 1)
                for k in range(KC):
                    cols = slice(k * P, (k + 1) * P)
                    ins = split_product(acc[k][:], (wd_hi[0:w, c, cols], wd_lo[0:w, c, cols]),
                                        (h_hi[0:w, slot[g]], h_lo[0:w, slot[g]]), c == 0, c == ITEMS - 1)
                    if c == ITEMS - 1:
                        ins.then_inc(acc_done, 1)
                    elif k == KC - 1:
                        ins.then_inc(down_done, 1)

            pe.wait_ge(warm_set, 1)
            for _ in range(WARM_UP):
                nc.tensor.matmul(bank[7][:], warm[:, 0:P], warm[:], start=True, stop=True)
            pe.wait_ge(ident_in, 16)
            norm_transposes("n1", 0, 0, 0)
            norm_transposes("n1", 0, 0, 1)
            layer_1(0, 0)
            norm_transposes("n1", 1, 1, 0)
            norm_transposes("n1", 1, 1, 1)
            layer_1(0, 1)
            layer_1(1, 0)
            layer_1(1, 1)
            for t in range(TT):
                layer_2(0, t)
            layer_2(1, 0)
            layer_2(1, 1)
            residual_transposes(0, 0)
            residual_transposes(0, 1)
            norm_transposes("n2", 2, 0, 0)
            norm_transposes("n2", 2, 0, 1)
            layer_2(1, 2)
            gate_or_up(0, False)
            gate_or_up(0, True)
            router(0)
            layer_2(1, 3)
            for g in range(1, N):
                gate_or_up(g, False)
                if g >= 3:
                    combine_weights(g)
                elif g == 2:
                    combine_weights(1)
                gate_or_up(g, True)
                if g == 1:
                    combine_transposes(0)
                if g == 2:
                    norm_transposes("n2", 3, 1, 0)
                    combine_weights(2)
                if g == 3:
                    norm_transposes("n2", 3, 1, 1)
                if g == 4:
                    residual_transposes(1, 0)
                if g == 5:
                    residual_transposes(1, 1)
                if g == place[1, 0] + 1:
                    router(1)
                if g == place[1, 1] - 1:
                    combine_transposes(1)
                if g == 3:
                    down(1)
                if g != 2 and items[g - 1] != (1, 0):
                    if items[g - 1] == (1, 1):
                        down(place[1, 0])
                    down(g - 1)
            down(N - 1)


def kernel(**inputs):
    import numpy as np
    import concourse.bacc as bacc
    from concourse.bass_utils import run_bass_kernel_spmd

    a = {k: np.asarray(v) for k, v in inputs.items()}
    gup, dp = a["L0_ffn_gate_up_proj"], a["L0_ffn_down_proj"]
    gate = gup[:, :I, :].reshape(E2 * I, D)
    up = gup[:, I:, :].reshape(E2 * I, D)

    def feature_major(*mats):
        return np.stack([m.T.reshape(KC, P, m.shape[0]).transpose(1, 0, 2) for m in mats], axis=2)

    router = a["L0_ffn_router_w"]
    shared = feature_major(np.concatenate([a["L0_ffn_shared_gate_w"], router, router, a["L0_ffn_shared_up_w"]]))
    routed = feature_major(gate, up).reshape(P, KC, 2, CH, P).transpose(0, 3, 1, 2, 4).reshape(P, CH * CW)
    ids = a["itok_BxS_13_99985"].reshape(TOKENS)
    sel = np.zeros((2, E2, CH * P), np.float32)
    sel[:, np.arange(CH * P) // I, np.arange(CH * P)] = 1.0
    arrays = {
        "x_d": a["x"].reshape(HALVES * TT, P, D).transpose(1, 0, 2),
        "idrow_d": ids,
        "idcol_d": ids.reshape(HALVES * TT, P).T,
        "ctx_d": a["ctx_2048"].transpose(2, 0, 1).reshape(KC, P, E1, D).transpose(1, 2, 0, 3),
        "bias_d": a["L0_ffn_e_bias"],
        "gu_d": np.concatenate([shared.reshape(P, SH), routed], axis=1),
        "wd0_d": a["L0_ffn_shared_down_w"].T,
        "wd_d": dp.transpose(0, 2, 1).reshape(CH, P, D).transpose(1, 0, 2).reshape(P, CH * D),
        "sel_d": sel.reshape(2 * E2, CH * P),
        "consts_d": np.concatenate([np.eye(P), np.tile(np.eye(E2), (P // E2, 1))], axis=1).astype(np.float32),
    }
    arrays = {k: np.ascontiguousarray(v) for k, v in arrays.items()}
    nc = bacc.Bacc("TRN2", target_bir_lowering=False, num_devices=1)
    aps = [nc.dram_tensor(k, v.shape, mybir.dt.from_np(v.dtype), kind="ExternalInput").ap() for k, v in arrays.items()]
    out = nc.dram_tensor("out_d", (P, KC, TOKENS), F32, kind="ExternalOutput").ap()
    build(nc, *aps, out)
    r = run_bass_kernel_spmd(nc, [arrays], core_ids=[0])
    got = r.results[0]["out_d"]
    return np.ascontiguousarray(got.transpose(1, 0, 2).reshape(D, TOKENS).T).reshape(a["x"].shape)
```

```python
from contextlib import ExitStack

import concourse.bass as bass
from concourse import mybir

F32 = mybir.dt.float32
F32R = mybir.dt.float32r
I32 = mybir.dt.int32
U8 = mybir.dt.uint8
BF16 = mybir.dt.bfloat16
ALU = mybir.AluOpType
ACT = mybir.ActivationFunctionType
AX = mybir.AxisListType

P = 128
TOKENS = 1024
D = 256
KC = D // P
HALF = 512
HALVES = TOKENS // HALF
TT = HALF // P
E1 = 4
VOCAB = 12500
PER_EXPERT = VOCAB // E1
EPS = 1e-5

E2 = 16
TOP = 4
I = 96
CH = E2 * I // P
ITEMS = CH + 1
RW = I
SHK = P + I
SH = KC * SHK
CW = 2 * KC * P
GU = SH + CH * CW
WARM_UP = 12
LAG = 2
SENTINEL = -3.0e38
MARK = 3.0e38

STAGE = 1024
SLOTS = 4
SPREADS = SLOTS * STAGE // HALF
RING = HALVES * KC


def weight_pieces():
    pieces = [("ctx", e * KC * D, KC * D) for e in range(E1)]
    pieces += [("gu", 0, SH)] + [("gu", c, STAGE) for c in range(SH, GU, STAGE)]
    pieces += [("wd0", 0, D)] + [("wd", c, STAGE) for c in range(0, CH * D, STAGE)]
    return pieces


def build(nc, x_d, xt_d, ids_d, ctx_d, bias_d, gu_d, wd0_d, wd_d, consts_d, out_d):
    pieces = weight_pieces()
    last_piece = {what: n for n, (what, _, _) in enumerate(pieces)}

    with ExitStack() as ctx:
        def sb(name, shape, dt=F32):
            return ctx.enter_context(nc.sbuf_tensor(name, shape, dt))

        def sem(name):
            return ctx.enter_context(nc.semaphore(name))

        x = sb("x", [P, HALVES * TT, D])
        xt = sb("xt", [P, KC, TOKENS])
        stage = sb("stage", [P, SLOTS, STAGE])
        ctx_hi = sb("ctx_hi", [P, E1, KC, D], F32R)
        ctx_lo = sb("ctx_lo", [P, E1, KC, D], F32R)
        gu_hi = sb("gu_hi", [P, GU], F32R)
        gu_lo = sb("gu_lo", [P, GU], F32R)
        wd_hi = sb("wd_hi", [P, ITEMS, D], F32R)
        wd_lo = sb("wd_lo", [P, ITEMS, D], F32R)
        consts_sb = sb("consts_sb", [P, P + E2])
        warm = sb("warm", [P, HALF], BF16)
        ids = sb("ids", [P, TOKENS], I32)
        beyond = sb("beyond", [P, E1 - 1, TOKENS], U8)
        stats = sb("stats", [P, TT, 6])
        meanvar = sb("meanvar", [P, TT, 2])
        vareps = sb("vareps", [P, TT])
        rstd = sb("rstd", [P, TT])
        power = sb("power", [P, TT])
        xn = sb("xn", [P, TT, D])
        xn_hi = sb("xn_hi", [P, HALVES, KC, HALF], F32R)
        xn_lo = sb("xn_lo", [P, HALVES, KC, HALF], F32R)
        act_sb = sb("act_sb", [P, 2, HALF])
        prod = sb("prod", [P, 2, HALF])
        hid = sb("hid", [P, 2, HALF])
        h_hi = sb("h_hi", [P, RING + 1, HALF], F32R)
        h_lo = sb("h_lo", [P, RING + 1, HALF], F32R)
        logits = sb("logits", [P, HALF])
        bias = sb("bias", [P, E2])
        scores = sb("scores", [P, TT, E2])
        biased = sb("biased", [P, TT, E2 + 4])
        best = sb("best", [P, TT, 8])
        marked = sb("marked", [P, TT, E2 + 4])
        weight = sb("weight", [P, TT, E2])
        wsum = sb("wsum", [P, TT])
        wsume = sb("wsume", [P, TT])
        winv = sb("winv", [P, TT])
        comb = sb("comb", [P, TT, E2])
        combt = sb("combt", [E2, HALVES, HALF])
        spread = stage[:].rearrange("p s (b t) -> p (s b) t", t=HALF)

        bank = [ctx.enter_context(nc.psum_tensor(f"bank{n}", [P, HALF], F32)) for n in range(8)]
        work = bank[0:4]
        acc = bank[6:8]

        x_in = [sem(f"x_in{n}") for n in range(3)]
        slot_in = [sem(f"slot_in{s}") for s in range(SLOTS)]
        ids_in, xt_in, bias_in, consts_in = sem("ids_in"), sem("xt_in"), sem("bias_in"), sem("consts_in")
        spread_in = [sem(f"spread_in{s}") for s in range(SPREADS)]
        out_written = sem("out_written")
        w_hi, w_lo = sem("w_hi"), sem("w_lo")
        consts, warm_set = sem("consts"), sem("warm_set")
        dstep = sem("dstep")
        varied, powered, normed = sem("varied"), sem("powered"), sem("normed")
        side_done = sem("side_done")
        xhi_done, xlo_done = sem("xhi_done"), sem("xlo_done")
        z_done, z_first, z_picked, z_silu = sem("z_done"), sem("z_first"), sem("z_picked"), sem("z_silu")
        h1_high, h1_done, x1_done = sem("h1_high"), sem("h1_done"), sem("x1_done")
        rw_done, logits_done, scored = sem("rw_done"), sem("logits_done"), sem("scored")
        combined, combt_done = sem("combined"), sem("combt_done")
        gate_done, up_done, silu_done, prod_done = sem("gate_done"), sem("up_done"), sem("silu_done"), sem("prod_done")
        hid_done, hhi_done, hlo_done, down_done = sem("hid_done"), sem("hhi_done"), sem("hlo_done"), sem("down_done")
        acc_done, out_ready = sem("acc_done"), sem("out_ready")

        side_order = [("n1", 0, 0, 4), ("n1", 0, 1, 5), ("n1", 1, 0, 4), ("n1", 1, 1, 5),
                      ("x1", 0, 0, 6), ("x1", 0, 1, 7), ("n2", 0, 0, 4), ("n2", 0, 1, 5),
                      ("router", 0, 0, 5), ("combt", 0, 0, 5),
                      ("x1", 1, 0, 4), ("x1", 1, 1, 5), ("n2", 1, 0, 4), ("n2", 1, 1, 5),
                      ("router", 1, 0, 5), ("combt", 1, 0, 5)]
        side_at = {u[:3]: n for n, u in enumerate(side_order)}

        def wait_side_read(eng, b, n):
            before = [u for u in side_order[:n] if u[3] == b]
            if not before:
                return
            what, h, k, _ = before[-1]
            if what in ("n1", "n2"):
                count = (HALVES * KC if what == "n2" else 0) + h * KC + k + 1
                eng.wait_ge(xhi_done, count)
                eng.wait_ge(xlo_done, count)
            elif what == "x1":
                eng.wait_ge(normed, TT * (HALVES + h + 1))
            elif what == "router":
                eng.wait_ge(scored, h + 1)
            else:
                eng.wait_ge(combt_done, h + 1)

        def side_bank(what, h, c):
            return bank[side_order[side_at[what, h, c]][3]]

        def widths(c):
            return I if c == 0 else P

        def gu_cols(c, k, up):
            if c == 0:
                at = k * SHK + up * P
                return slice(at, at + I)
            at = SH + (c - 1) * CW + (k * 2 + up) * P
            return slice(at, at + P)

        def outs(h):
            last = h == HALVES - 1
            parts = [2 if last and k == KC - 1 else 1 for k in range(KC)]
            return [(k, slice(n * HALF // parts[k], (n + 1) * HALF // parts[k])) for k in range(KC) for n in range(parts[k])]

        def parts_of_chunk(c):
            at = (c - 1) * P
            return [(max(e * I, at) - at, min((e + 1) * I, at + P) - at, e)
                    for e in range(at // I, (at + P - 1) // I + 1)]

        def gu_piece(c):
            return last_piece["ctx"] + 1 + (0 if c == 0 else 1 + (c - 1) * CW // STAGE)

        def wd_piece(c):
            return last_piece["wd0"] + (0 if c == 0 else 1 + (c - 1) * D // STAGE)

        mixes = [(1, 0, 0), (1, 0, 1), (1, 1, 0), (2, 0, 0), (2, 0, 1), (1, 1, 1), (2, 1, 0), (2, 1, 1)]
        mixed = {mix: n for n, mix in enumerate(mixes)}

        def wait_mixed(eng, n):
            layer, h, m = mixes[n]
            eng.wait_ge(h1_done if layer == 1 else x1_done, h * KC + m + 1)

        early = 8
        items = [(0, c) for c in range(early + 1)] + [(1, 0)]
        items += [(0, c) for c in range(early + 1, ITEMS)] + [(1, c) for c in range(1, ITEMS)]
        N = len(items)
        place = {item: g for g, item in enumerate(items)}
        downs = [place[h, c] for h in range(HALVES) for c in range(ITEMS)]
        downs_at = {g: [g] for g in range(N)}
        downs_at[place[1, 0]] = []
        downs_at[place[1, 1]] = [place[1, 0], place[1, 1]]
        ring = [g for g in range(N) if g != place[1, 0]]
        slot = {g: n % RING for n, g in enumerate(ring)} | {place[1, 0]: RING}
        former = {g: ring[n - RING] for n, g in enumerate(ring) if n >= RING}

        def routed(g):
            return sum(c > 0 for _, c in items[:g + 1])

        def wait_down(eng, g):
            h, c = items[g]
            if c == ITEMS - 1:
                eng.wait_ge(acc_done, (h + 1) * KC)
            else:
                eng.wait_ge(down_done, downs.index(g) + 1 - h)

        def gate_bank(g):
            return acc[0] if g == 0 else work[2 * ((g + 1) % 2)]

        def up_bank(g):
            return acc[1] if g == 0 else work[2 * ((g + 1) % 2) + 1]

        def piece_aps(n):
            what, at, cols = pieces[n]
            st = stage[:, n % SLOTS, 0:cols]
            if what == "ctx":
                e = at // (KC * D)
                st = st.rearrange("p (k f) -> p k f", k=KC)
                return ctx_d[:, e], st, ctx_hi[:, e], ctx_lo[:, e]
            if what == "gu":
                return gu_d[:, at:at + cols], st, gu_hi[:, at:at + cols], gu_lo[:, at:at + cols]
            if what == "wd0":
                st = stage[0:I, n % SLOTS, 0:cols]
                return wd0_d, st, wd_hi[0:I, 0], wd_lo[0:I, 0]
            hi = wd_hi[:, 1:, :].rearrange("p c d -> p (c d)")[:, at:at + cols]
            lo = wd_lo[:, 1:, :].rearrange("p c d -> p (c d)")[:, at:at + cols]
            return wd_d[:, at:at + cols], st, hi, lo

        block = ctx.enter_context(nc.Block())

        @block.sync
        def _(sp):
            def load_piece(n):
                if n >= SLOTS:
                    sp.wait_ge(w_hi, n - SLOTS + 1)
                    sp.wait_ge(w_lo, n - SLOTS + 1)
                dram, st, _, _ = piece_aps(n)
                sp.dma_start(st, dram).then_inc(slot_in[n % SLOTS], 16)

            sp.dma_start(x[:, 0:TT // 2], x_d[:, 0:TT // 2]).then_inc(x_in[0], 16)
            sp.dma_start(x[:, TT // 2:TT], x_d[:, TT // 2:TT]).then_inc(x_in[1], 16)
            load_piece(0)
            sp.dma_start(consts_sb[:], consts_d).then_inc(consts_in, 16)
            for n in range(1, SLOTS):
                load_piece(n)
            sp.dma_start(x[:, TT:], x_d[:, TT:]).then_inc(x_in[2], 16)
            sp.dma_start(ids[:], ids_d.partition_broadcast(P)).then_inc(ids_in, 16)
            for n in range(SLOTS, len(pieces)):
                load_piece(n)
                if n == 6:
                    sp.dma_start(xt[:], xt_d).then_inc(xt_in, 16)
                    sp.dma_start(bias[:], bias_d.partition_broadcast(P)).then_inc(bias_in, 16)

            def spread_combine_weights(h, c):
                n = h * CH + c - 1
                if c == 1:
                    sp.wait_ge(combt_done, h + 1)
                if n == 0:
                    sp.wait_ge(w_hi, len(pieces))
                    sp.wait_ge(w_lo, len(pieces))
                if n >= SPREADS:
                    sp.wait_ge(prod_done, n - SPREADS + 1)
                for first, last, e in parts_of_chunk(c):
                    row = combt[e:e + 1, h].unsqueeze(1).to_broadcast([1, last - first, HALF])
                    sp.dma_start(spread[first:last, n % SPREADS], row).then_inc(spread_in[n % SPREADS], 16)

            def write_output(h):
                for n, (k, t) in enumerate(outs(h)):
                    sp.wait_ge(out_ready, h * KC + n + 1)
                    s = slice(h * HALF + t.start, h * HALF + t.stop)
                    sp.dma_start(out_d[:, k, s], xt[:, k, s]).then_inc(out_written, 16)

            for h in range(HALVES):
                for c in range(1, ITEMS):
                    spread_combine_weights(h, c)
                    if (h, c) == (1, SPREADS):
                        write_output(0)
            write_output(1)
            sp.wait_ge(out_written, 16 * sum(len(outs(h)) for h in range(HALVES)))

        @block.gpsimd
        def _(pool):
            nc.gpsimd.memset(warm[:], 0.0).then_inc(warm_set, 1)
            nc.gpsimd.memset(power[:], -0.5).then_inc(consts, 1)
            nc.gpsimd.memset(biased[:, :, E2:], SENTINEL).then_inc(consts, 1)
            pool.wait_ge(consts, 2)

            def low_part(n):
                pool.wait_ge(w_hi, n + 1)
                pool.wait_ge(slot_in[n % SLOTS], 16 * (n // SLOTS + 1))
                _, st, hi, lo = piece_aps(n)
                nc.gpsimd.tensor_tensor(lo, st, hi.bitcast(F32), ALU.subtract).then_inc(w_lo, 1)

            def rstd_of(n, cols=slice(0, TT)):
                pool.wait_ge(varied, n + 1)
                if n >= 2:
                    pool.wait_ge(normed, TT * (n - 1))
                nc.gpsimd.tensor_tensor(rstd[:, cols], vareps[:, cols], power[:, cols], ALU.pow).then_inc(powered, 1)

            rstd_of(0, slice(0, TT // 2))
            rstd_of(1, slice(TT // 2, TT))
            for n in range(E1):
                low_part(n)
            rstd_of(2)
            for n in range(E1, len(pieces)):
                if n == last_piece["wd"] - 1:
                    rstd_of(3)
                low_part(n)
            rstd_of(4)

        @block.scalar
        def _(act):
            def high_part(n):
                act.wait_ge(slot_in[n % SLOTS], 16 * (n // SLOTS + 1))
                _, st, hi, _ = piece_aps(n)
                nc.scalar.activation(hi, st, ACT.Copy).then_inc(w_hi, 1)

            def x_high(what, h, k):
                act.wait_ge(side_done, side_at[what, h, k] + 1)
                if what == "n2":
                    act.wait_ge(z_done, (mixed[1, h, KC - 1] + 1) * E1)
                nc.scalar.activation(xn_hi[:, h, k], side_bank(what, h, k)[:], ACT.Copy).then_inc(xhi_done, 1)

            def first_z(n):
                act.wait_ge(z_done, n * E1 + 1)
                if n >= 2:
                    wait_mixed(act, n - 2)
                nc.scalar.activation(prod[:, n % 2], work[0][:], ACT.Copy).then_inc(z_first, 1)

            def silu_z(n):
                act.wait_ge(z_picked, (n + 1) * (E1 - 1))
                if n >= 2:
                    wait_mixed(act, max(k for k in range(n) if mixes[k][0] == 1 and k % 2 == n % 2))
                nc.scalar.activation(act_sb[:, n % 2], prod[:, n % 2], ACT.Silu).then_inc(z_silu, 1)

            def score(h):
                act.wait_ge(side_done, side_at["router", h, 0] + 1)
                if h:
                    act.wait_ge(combined, h)
                nc.scalar.activation(scores[:].rearrange("p t e -> p (t e)"),
                                     side_bank("router", h, 0)[:, 0:TT * E2], ACT.Sigmoid).then_inc(scored, 1)

            def combine_rows(h):
                act.wait_ge(side_done, side_at["combt", h, 0] + 1)
                nc.scalar.activation(combt[:, h], side_bank("combt", h, 0)[0:E2, :], ACT.Copy).then_inc(combt_done, 1)

            def router_logits(h):
                act.wait_ge(gate_done, place[h, 0] + 1)
                if h:
                    act.wait_ge(side_done, side_at["router", h - 1, 0] + 1)
                nc.scalar.activation(logits[RW:, :], gate_bank(place[h, 0])[RW:, :], ACT.Copy).then_inc(logits_done, 1)

            def silu_gate(g):
                w = widths(items[g][1])
                act.wait_ge(gate_done, g + 1)
                if g >= 2:
                    act.wait_ge(hid_done, g - 1)
                else:
                    act.wait_ge(h1_done, HALVES * KC)
                nc.scalar.activation(act_sb[0:w, g % 2], gate_bank(g)[0:w, :], ACT.Silu).then_inc(silu_done, 1)

            def hid_high(g):
                w = widths(items[g][1])
                act.wait_ge(hid_done, g + 1)
                if g in former:
                    wait_down(act, former[g])
                elif g < RING:
                    act.wait_ge(z_done, (mixed[2, g // KC, KC - 1] + 1) * E1)
                nc.scalar.activation(h_hi[0:w, slot[g]], hid[0:w, g % 2], ACT.Copy).then_inc(hhi_done, 1)

            nc.scalar.preload_act_table(ACT.Silu)
            high_part(0)
            high_part(1)
            high_part(2)
            x_high("n1", 0, 0)
            x_high("n1", 0, 1)
            high_part(3)
            first_z(0)
            x_high("n1", 1, 0)
            x_high("n1", 1, 1)
            high_part(4)
            silu_z(0)
            high_part(5)
            first_z(1)
            high_part(6)
            silu_z(1)
            first_z(2)
            high_part(7)
            high_part(8)
            silu_z(2)
            first_z(3)
            high_part(9)
            high_part(10)
            first_z(4)
            high_part(11)
            high_part(12)
            high_part(13)
            first_z(5)
            high_part(14)
            silu_z(5)
            for n in range(15, len(pieces)):
                high_part(n)
            x_high("n2", 0, 0)
            x_high("n2", 0, 1)
            first_z(6)
            router_logits(0)
            silu_gate(0)
            score(0)
            hid_high(0)
            first_z(7)
            for g in range(1, N):
                if g == place[1, 0] - 1:
                    x_high("n2", 1, 0)
                    x_high("n2", 1, 1)
                if g == place[1, 0] + 2:
                    score(1)
                if g == place[1, 0]:
                    router_logits(1)
                silu_gate(g)
                if g == 1:
                    combine_rows(0)
                if g == place[1, 1] - 1:
                    combine_rows(1)
                hid_high(g)

        @block.vector
        def _(dve):
            steps = [0]

            def step(ins):
                steps[0] += 1
                ins.then_inc(dstep, 1)
                return steps[0]

            def tile_to_norm(n, t):
                if n < HALVES:
                    return x[:, n * TT + t]
                at = t % (TT // KC) * D
                return side_bank("x1", n - HALVES, t // (TT // KC))[:, at:at + D]

            def tile_stats(n, t):
                if n >= HALVES:
                    dve.wait_ge(side_done, side_at["x1", n - HALVES, t // (TT // KC)] + 1)
                step(nc.vector.bn_stats(stats[:, t], tile_to_norm(n, t)))

            def layer_norm_vars(tiles=range(TT)):
                dve.wait_ge(dstep, steps[0])
                for t in tiles:
                    step(nc.vector.bn_aggr(meanvar[:, t], stats[:, t]))
                dve.wait_ge(dstep, steps[0])
                s = slice(tiles[0], tiles[-1] + 1)
                nc.vector.tensor_scalar(vareps[:, s], meanvar[:, s, 1], EPS, None, ALU.add).then_inc(varied, 1)

            def layer_norm_apply(n, tiles=range(TT)):
                dve.wait_ge(powered, n + 2 if n > 0 or tiles[0] > 0 else 1)
                if n > 0:
                    what, hh = [("n1", 0), ("n1", 1), ("n2", 0)][n - 1]
                    dve.wait_ge(side_done, side_at[what, hh, 1] + 1)
                for t in tiles:
                    nc.vector.tensor_scalar(xn[:, t], tile_to_norm(n, t), meanvar[:, t, 0:1], rstd[:, t:t + 1],
                                            ALU.subtract, ALU.mult).then_inc(normed, 1)

            def x_low(what, h, k):
                n = (HALVES * KC if what == "n2" else 0) + h * KC + k
                dve.wait_ge(xhi_done, n + 1)
                dve.wait_ge(side_done, side_at[what, h, k] + 1)
                nc.vector.tensor_tensor(xn_lo[:, h, k], side_bank(what, h, k)[:], xn_hi[:, h, k].bitcast(F32),
                                        ALU.subtract).then_inc(xlo_done, 1)

            def thresholds(h, experts=range(1, E1)):
                dve.wait_ge(ids_in, 16)
                for e in experts:
                    last = step(nc.vector.tensor_scalar(beyond[:, e - 1, h * HALF:(h + 1) * HALF],
                                                        ids[:, h * HALF:(h + 1) * HALF],
                                                        float(e * PER_EXPERT), None, ALU.is_ge))
                return last

            def pick(n, masked, experts=range(1, E1)):
                h = mixes[n][1]
                dve.wait_ge(z_first, n + 1)
                dve.wait_ge(dstep, masked)
                for e in experts:
                    dve.wait_ge(z_done, n * E1 + e + 1)
                    if e > 1:
                        dve.wait_ge(z_picked, n * (E1 - 1) + e - 1)
                    nc.vector.copy_predicated(prod[:, n % 2], beyond[:, e - 1, h * HALF:(h + 1) * HALF],
                                              work[e][:]).then_inc(z_picked, 1)

            def hidden_1(n):
                _, h, m = mixes[n]
                b = h * KC + m
                dve.wait_ge(z_silu, b + 1)
                last = step(nc.vector.tensor_tensor(hid[:, b % 2], act_sb[:, n % 2], prod[:, n % 2], ALU.mult))
                dve.wait_ge(dstep, last)
                nc.vector.tensor_scalar(h_hi[:, b], hid[:, b % 2], 1.0, None, ALU.mult).then_inc(h1_high, 1)
                dve.wait_ge(h1_high, b + 1)
                nc.vector.tensor_tensor(h_lo[:, b], hid[:, b % 2], h_hi[:, b].bitcast(F32),
                                        ALU.subtract).then_inc(h1_done, 1)

            def add_block_1(n):
                _, h, m = mixes[n]
                dve.wait_ge(xt_in, 16)
                dve.wait_ge(z_picked, (n + 1) * (E1 - 1))
                o = xt[:, m, h * HALF:(h + 1) * HALF]
                nc.vector.tensor_tensor(o, prod[:, n % 2], o, ALU.add).then_inc(x1_done, 1)

            def router_low_rows():
                n = gu_piece(0)
                dve.wait_ge(w_hi, n + 1)
                dve.wait_ge(w_lo, n + 1)
                hi, lo = (w[:, 0:SH].rearrange("p (k c) -> p k c", k=KC) for w in (gu_hi, gu_lo))
                nc.vector.tensor_copy(hi[:, :, RW + E2:RW + 2 * E2], lo[:, :, RW:RW + E2].bitcast(F32)).then_inc(rw_done, 1)

            def mark_best(h):
                dve.wait_ge(scored, h + 1)
                dve.wait_ge(consts, 2)
                dve.wait_ge(bias_in, 16)
                last = step(nc.vector.tensor_tensor(
                    biased[:, :, 0:E2], scores[:], bias[:].unsqueeze(1).to_broadcast([P, TT, E2]), ALU.add))
                dve.wait_ge(dstep, last)
                for t in range(TT):
                    last = step(nc.vector.max(best[:, t], biased[:, t, 0:E2]))
                dve.wait_ge(dstep, last)
                last = step(nc.vector.memset(best[:, :, TOP:], SENTINEL))
                dve.wait_ge(dstep, last)
                for t in range(TT):
                    last = step(nc.vector.match_replace(marked[:, t], best[:, t], biased[:, t], MARK))
                return last

            def normalise_scores(h, marks):
                if h:
                    dve.wait_ge(side_done, side_at["combt", h - 1, 0] + 1)
                dve.wait_ge(dstep, marks)
                last = step(nc.vector.scalar_tensor_tensor(out=weight[:], in0=marked[:, :, 0:E2], scalar=MARK, in1=scores[:],
                                                           op0=ALU.is_equal, op1=ALU.mult))
                dve.wait_ge(dstep, last)
                last = step(nc.vector.tensor_reduce(wsum[:], weight[:], AX.X, ALU.add))
                dve.wait_ge(dstep, last)
                last = step(nc.vector.tensor_scalar(wsume[:], wsum[:], 1e-20, None, ALU.add))
                dve.wait_ge(dstep, last)
                last = step(nc.vector.reciprocal(winv[:], wsume[:]))
                dve.wait_ge(dstep, last)
                nc.vector.tensor_tensor(comb[:], weight[:], winv[:].unsqueeze(2).to_broadcast([P, TT, E2]),
                                        ALU.mult).then_inc(combined, 1)

            def product(g):
                if items[g][1] == 0:
                    return
                dve.wait_ge(silu_done, g + 1)
                n = routed(g) - 1
                dve.wait_ge(spread_in[n % SPREADS], 16 * sum(
                    len(parts_of_chunk(m % CH + 1)) for m in range(n % SPREADS, n + 1, SPREADS)))
                if g < 2:
                    dve.wait_ge(x1_done, HALVES * KC)
                nc.vector.tensor_tensor(prod[:, g % 2], act_sb[:, g % 2], spread[:, n % SPREADS],
                                        ALU.mult).then_inc(prod_done, 1)

            def hidden_2(g):
                w = widths(items[g][1])
                if items[g][1] == 0:
                    dve.wait_ge(silu_done, g + 1)
                else:
                    dve.wait_ge(prod_done, routed(g))
                dve.wait_ge(up_done, g + 1)
                if g >= 2:
                    dve.wait_ge(hhi_done, g - 1)
                src = (act_sb if items[g][1] == 0 else prod)[0:w, g % 2]
                nc.vector.tensor_tensor(hid[0:w, g % 2], src, up_bank(g)[0:w, :], ALU.mult).then_inc(hid_done, 1)

            def hid_low(g):
                w = widths(items[g][1])
                dve.wait_ge(hhi_done, g + 1)
                nc.vector.tensor_tensor(h_lo[0:w, slot[g]], hid[0:w, g % 2], h_hi[0:w, slot[g]].bitcast(F32),
                                        ALU.subtract).then_inc(hlo_done, 1)

            def output(h):
                for n, (k, t) in enumerate(outs(h)):
                    dve.wait_ge(acc_done, h * KC + k + 1)
                    o = xt[:, k, h * HALF + t.start:h * HALF + t.stop]
                    nc.vector.tensor_tensor(o, acc[k][:, t], o, ALU.add).then_inc(out_ready, 1)

            for n, tiles in enumerate((range(TT // 2), range(TT // 2, TT))):
                dve.wait_ge(x_in[n], 16)
                for t in tiles:
                    tile_stats(0, t)
                layer_norm_vars(tiles)
            for n, tiles in enumerate((range(TT // 2), range(TT // 2, TT))):
                layer_norm_apply(0, tiles)
            x_low("n1", 0, 0)
            x_low("n1", 0, 1)
            dve.wait_ge(x_in[2], 16)
            for t in range(TT):
                tile_stats(1, t)
            layer_norm_vars()
            masked = [thresholds(0)]
            layer_norm_apply(1)
            pick(0, masked[0])
            x_low("n1", 1, 0)
            x_low("n1", 1, 1)
            hidden_1(0)
            for e in range(1, E1):
                pick(1, masked[0], [e])
                last = thresholds(1, [e])
            masked.append(last)
            hidden_1(1)
            pick(2, masked[1])
            hidden_1(2)
            router_low_rows()
            for n in (3, 4):
                pick(n, masked[0])
                add_block_1(n)
            pick(5, masked[1], [1])
            for t in range(TT):
                tile_stats(2, t)
            layer_norm_vars()
            pick(5, masked[1], [2, 3])
            layer_norm_apply(2)
            hidden_1(5)
            x_low("n2", 0, 0)
            x_low("n2", 0, 1)
            pick(6, masked[1])
            add_block_1(6)
            hidden_2(0)
            hid_low(0)
            marks = mark_best(0)
            pick(7, masked[1], [1])
            normalise_scores(0, marks)
            pick(7, masked[1], [2, 3])
            add_block_1(7)
            for g in range(1, N):
                if g == place[1, 0] - 1:
                    x_low("n2", 1, 0)
                    x_low("n2", 1, 1)
                product(g)
                if g == place[1, 0] + 2:
                    marks = mark_best(1)
                hidden_2(g)
                if g == place[1, 1] + 1:
                    output(0)
                hid_low(g)
                if g == 4:
                    for t in range(TT):
                        tile_stats(3, t)
                    layer_norm_vars()
                if g == 5:
                    layer_norm_apply(3)
                if g == place[1, 0] + 2:
                    normalise_scores(1, marks)
            output(1)

        @block.tensor
        def _(pe):
            def side_wait(what, h, c):
                u = side_at[what, h, c]
                b = side_order[u][3]
                wait_side_read(pe, b, u)
                return bank[b]

            def norm_transposes(what, n, h):
                banks = [side_wait(what, h, k) for k in range(KC)]
                for t in range(TT):
                    pe.wait_ge(normed, TT * n + t + 1)
                    for k in range(KC):
                        ins = nc.tensor.transpose(banks[k][:, t * P:(t + 1) * P], xn[:, t, k * P:(k + 1) * P],
                                                  consts_sb[:, 0:P])
                        if t == TT - 1:
                            ins.then_inc(side_done, 1)

            def x1_transposes(h, pair):
                pe.wait_ge(x1_done, (h + 1) * KC)
                b = side_wait("x1", h, pair)
                for t in range(TT // KC):
                    at = h * HALF + (pair * (TT // KC) + t) * P
                    for k in range(KC):
                        ins = nc.tensor.transpose(b[:, t * D + k * P:t * D + (k + 1) * P], xt[:, k, at:at + P],
                                                  consts_sb[:, 0:P])
                ins.then_inc(side_done, 1)

            def mix(n, between=lambda: None, after=0, late=False):
                layer, h, m = mixes[n]
                f = slice(m * P, (m + 1) * P)
                if layer == 1:
                    parts = [(xn_hi[:, h, k], xn_lo[:, h, k]) for k in range(KC)]
                else:
                    parts = [(h_hi[:, h * KC + k], h_lo[:, h * KC + k]) for k in range(KC)]

                def operands(k, low):
                    if layer == 1:
                        pe.wait_ge(xlo_done if low else xhi_done, h * KC + k + 1)
                    else:
                        pe.wait_ge(h1_done if low else h1_high, h * KC + k + 1)

                def bank_read(e):
                    if n > 0 and e == 0:
                        pe.wait_ge(z_first, n)
                    elif n > 0:
                        pe.wait_ge(z_picked, (n - 1) * (E1 - 1) + e)

                def term(e, k, a, b, start=False, stop=False):
                    return nc.tensor.matmul(work[e][:], (ctx_hi, ctx_lo)[a][:, e, k, f], parts[k][b], start=start, stop=stop)

                if layer == 2 and m == 0:
                    for e in range(E1):
                        if e == 0:
                            operands(0, False)
                        bank_read(e)
                        term(e, 0, 0, 0, start=True)
                        term(e, 0, 1, 0)
                        if e == 0:
                            operands(0, True)
                        term(e, 0, 0, 1)
                    between()
                    operands(1, False)
                    groups = [range(E1)] if late else [[e] for e in range(E1)]
                    for group in groups:
                        for e in group:
                            term(e, 1, 0, 0)
                            term(e, 1, 1, 0)
                        if group[0] == 0:
                            operands(1, True)
                        for e in group:
                            term(e, 1, 0, 1, stop=True).then_inc(z_done, 1)
                    return
                for e in range(E1):
                    if n == 0:
                        pe.wait_ge(w_hi, e + 1)
                        pe.wait_ge(w_lo, e + 1)
                    bank_read(e)
                    for i, (a, b) in enumerate(((0, 0), (1, 0), (0, 1))):
                        for k in range(KC):
                            if e == 0 and a == 0:
                                operands(k, b == 1)
                            ins = term(e, k, a, b, start=(i == 0 and k == 0), stop=(i == 2 and k == KC - 1))
                    ins.then_inc(z_done, 1)
                    if e == after:
                        between()

            def router(h):
                pe.wait_ge(logits_done, h + 1)
                b = side_wait("router", h, 0)
                for t in range(TT):
                    ins = nc.tensor.matmul(b[:, t * E2:(t + 1) * E2], logits[RW:, t * P:(t + 1) * P],
                                           consts_sb[RW:, P:], start=True, stop=True)
                ins.then_inc(side_done, 1)

            def combine_transposes(h):
                pe.wait_ge(combined, h + 1)
                b = side_wait("combt", h, 0)
                for t in range(TT):
                    ins = nc.tensor.transpose(b[0:E2, t * P:(t + 1) * P], comb[:, t], consts_sb[:, 0:P])
                ins.then_inc(side_done, 1)

            def gate_or_up(g, up):
                h, c = items[g]
                w = widths(c)
                if h == 0:
                    n = gu_piece(c)
                    pe.wait_ge(w_hi, n + 1)
                    pe.wait_ge(w_lo, n + 1)
                if c == 0:
                    pe.wait_ge(rw_done, 1)
                    pe.wait_ge(xhi_done, (HALVES + h + 1) * KC)
                    pe.wait_ge(xlo_done, (HALVES + h + 1) * KC)
                if g == 1 and not up:
                    pe.wait_ge(z_first, len(mixes))
                    pe.wait_ge(z_picked, len(mixes) * (E1 - 1) - 2)
                elif g == 2 and not up:
                    pe.wait_ge(z_picked, len(mixes) * (E1 - 1))
                elif g > 2 and up:
                    pe.wait_ge(hid_done, g - 1)
                elif g > 2:
                    pe.wait_ge(silu_done, g - 1)
                    if items[g - 2][1] == 0:
                        pe.wait_ge(logits_done, items[g - 2][0] + 1)
                out = (up_bank if up else gate_bank)(g)
                for k in range(KC):
                    cols = gu_cols(c, k, up)
                    wide = slice(cols.start, cols.start + P) if c == 0 and not up else cols
                    rows = wide.stop - wide.start
                    nc.tensor.matmul(out[0:rows, :], gu_hi[:, wide], xn_hi[:, h, k], start=(k == 0), stop=False)
                    nc.tensor.matmul(out[0:w, :], gu_lo[:, cols], xn_hi[:, h, k], start=False, stop=False)
                    ins = nc.tensor.matmul(out[0:rows, :], gu_hi[:, wide], xn_lo[:, h, k], start=False, stop=(k == KC - 1))
                ins.then_inc(up_done if up else gate_done, 1)

            def down(g, outputs=range(KC)):
                h, c = items[g]
                w = widths(c)
                if h == 0:
                    n = wd_piece(c)
                    pe.wait_ge(w_hi, n + 1)
                    pe.wait_ge(w_lo, n + 1)
                if g == 0:
                    pe.wait_ge(logits_done, 1)
                elif c == 0:
                    pe.wait_ge(out_ready, h * KC)
                hi, lo = h_hi[0:w, slot[g]], h_lo[0:w, slot[g]]
                for k in outputs:
                    cols = slice(k * P, (k + 1) * P)
                    pe.wait_ge(hhi_done, g + 1)
                    nc.tensor.matmul(acc[k][:], wd_hi[0:w, c, cols], hi, start=(c == 0), stop=False)
                    nc.tensor.matmul(acc[k][:], wd_lo[0:w, c, cols], hi, start=False, stop=False)
                    pe.wait_ge(hlo_done, g + 1)
                    ins = nc.tensor.matmul(acc[k][:], wd_hi[0:w, c, cols], lo, start=False, stop=(c == ITEMS - 1))
                    if c == ITEMS - 1:
                        ins.then_inc(acc_done, 1)
                if c < ITEMS - 1 and KC - 1 in outputs:
                    ins.then_inc(down_done, 1)

            pe.wait_ge(warm_set, 1)
            for _ in range(WARM_UP):
                nc.tensor.matmul(bank[7][:], warm[:, 0:P], warm[:], start=True, stop=True)
            pe.wait_ge(consts_in, 16)
            norm_transposes("n1", 0, 0)
            mix(0)
            mix(1, lambda: norm_transposes("n1", 1, 1))
            for n in range(2, 5):
                mix(n)
            mix(5, lambda: (x1_transposes(0, 0), x1_transposes(0, 1)), 1)
            mix(6, lambda: norm_transposes("n2", 2, 0), late=True)
            gate_or_up(0, False)
            gate_or_up(0, True)
            router(0)
            mix(7)
            for g in range(1, N):
                gate_or_up(g, False)
                if g == 1:
                    combine_transposes(0)
                gate_or_up(g, True)
                if g == 2:
                    x1_transposes(1, 0)
                    x1_transposes(1, 1)
                if g == place[1, 0] - 2:
                    norm_transposes("n2", 3, 1)
                if g == place[1, 0] + 1:
                    router(1)
                if g == place[1, 1] - 1:
                    combine_transposes(1)
                for n in downs_at[g - LAG] if g >= LAG else []:
                    down(n)
            for k in range(KC):
                for n in range(N - LAG, N):
                    down(n, [k])


def kernel(**inputs):
    import numpy as np
    import concourse.bacc as bacc
    from concourse.bass_utils import run_bass_kernel_spmd

    a = {k: np.asarray(v) for k, v in inputs.items()}
    gup, dp = a["L0_ffn_gate_up_proj"], a["L0_ffn_down_proj"]
    gate = gup[:, :I, :].reshape(E2 * I, D)
    up = gup[:, I:, :].reshape(E2 * I, D)

    def feature_major(*mats):
        return np.stack([m.T.reshape(KC, P, m.shape[0]).transpose(1, 0, 2) for m in mats], axis=2)

    router = a["L0_ffn_router_w"]
    shared = feature_major(np.concatenate([a["L0_ffn_shared_gate_w"], router, router, a["L0_ffn_shared_up_w"]]))
    routed = feature_major(gate, up).reshape(P, KC, 2, CH, P).transpose(0, 3, 1, 2, 4).reshape(P, CH * CW)
    ids = a["itok_BxS_13_99985"].reshape(TOKENS)
    arrays = {
        "x_d": a["x"].reshape(HALVES * TT, P, D).transpose(1, 0, 2),
        "xt_d": a["x"].reshape(TOKENS, KC, P).transpose(2, 1, 0),
        "ids_d": ids,
        "ctx_d": a["ctx_2048"].transpose(2, 0, 1).reshape(KC, P, E1, D).transpose(1, 2, 0, 3),
        "bias_d": a["L0_ffn_e_bias"],
        "gu_d": np.concatenate([shared.reshape(P, SH), routed], axis=1),
        "wd0_d": a["L0_ffn_shared_down_w"].T,
        "wd_d": dp.transpose(0, 2, 1).reshape(CH, P, D).transpose(1, 0, 2).reshape(P, CH * D),
        "consts_d": np.concatenate([np.eye(P), np.tile(np.eye(E2), (P // E2, 1))], axis=1).astype(np.float32),
    }
    arrays = {k: np.ascontiguousarray(v) for k, v in arrays.items()}
    nc = bacc.Bacc("TRN2", target_bir_lowering=False, num_devices=1)
    aps = [nc.dram_tensor(k, v.shape, mybir.dt.from_np(v.dtype), kind="ExternalInput").ap() for k, v in arrays.items()]
    out = nc.dram_tensor("out_d", (P, KC, TOKENS), F32, kind="ExternalOutput").ap()
    build(nc, *aps, out)
    r = run_bass_kernel_spmd(nc, [arrays], core_ids=[0])
    got = r.results[0]["out_d"]
    return np.ascontiguousarray(got.transpose(1, 0, 2).reshape(D, TOKENS).T).reshape(a["x"].shape)
```
